# Optimizing a Trainium2 kernel written in Bass

```python
import numpy as np
import jax
import jax.numpy as jnp

def _softmax(x, axis=-1):
    return jax.nn.softmax(x, axis=axis)

def _gelu(x):
    return jax.nn.gelu(x, approximate=True)

def _silu(x):
    return jax.nn.silu(x)

def _sigmoid(x):
    return jax.nn.sigmoid(x)

def _layernorm(x, axis=-1, eps=1e-05):
    m = jnp.mean(x, axis=axis, keepdims=True)
    v = jnp.var(x, axis=axis, keepdims=True)
    return (x - m) / jnp.sqrt(v + eps)

def _scatter_add(tgt, idx, src, axis=0):
    return tgt.at[idx].add(src)

def _segment_sum(src, seg, n):
    return jax.ops.segment_sum(src, seg, n)
kernel_name = 'mk_vit_tower_cls_d4_tok_img1024_r4_e944b1'

def setup_inputs(seed: int=0):
    np.random.seed(seed)
    _w = jnp.asarray

    def _rec_inputs():
        import jax
        import jax.numpy as jnp
        _rk = jax.random.key(seed)
        x = -0.000392918 + 0.999932 * jax.random.normal(jax.random.fold_in(_rk, 1), (8, 256, 256, 1), jnp.float32)
        cls_tok = 0.02 * jax.random.normal(jax.random.fold_in(_rk, 5), (1, 1, 256), jnp.float32)
        return (x, cls_tok)
    x, cls_tok = _rec_inputs()

    def _L0_tok_setup():
        import jax, jax.numpy as jnp
        import numpy as np
        INV_SQRT2 = 0.7071067811865476
        LEVEL = 3

        def _split(x, axis):
            ax = axis % x.ndim
            sl0 = [slice(None)] * x.ndim
            sl0[ax] = slice(0, None, 2)
            sl1 = [slice(None)] * x.ndim
            sl1[ax] = slice(1, None, 2)
            x0, x1 = (x[tuple(sl0)], x[tuple(sl1)])
            return ((x0 + x1) * INV_SQRT2, (x0 - x1) * INV_SQRT2)

        def _merge(lo, hi, axis):
            ax = axis % lo.ndim
            e = (lo + hi) * INV_SQRT2
            o = (lo - hi) * INV_SQRT2
            s = jnp.stack([e, o], axis=ax + 1)
            shape = list(lo.shape)
            shape[ax] *= 2
            return s.reshape(shape)

        def _dwt2(x):
            lo, hi = _split(x, -1)
            a, h = _split(lo, -2)
            v, d = _split(hi, -2)
            return (a, h, v, d)

        def _idwt2(a, h, v, d):
            lo = _merge(a, h, -2)
            hi = _merge(v, d, -2)
            return _merge(lo, hi, -1)
        key = jax.random.key(seed)
        ks = jax.random.split(key, 8)
        B, H, W = (16, 256, 256)
        x = jax.random.normal(ks[0], (B, H, W, 1), dtype=jnp.float32)
        na = H // 8 * (W // 8)
        n2 = H // 4 * (W // 4)
        n1 = H // 2 * (W // 2)
        scale = 0.02
        Wa = jax.random.normal(ks[1], (na, 1), dtype=jnp.float32) * scale
        ba = jnp.zeros((1,), jnp.float32)
        Wd1 = jax.random.normal(ks[2], (3 * na, 3), dtype=jnp.float32) * scale
        bd1 = jnp.zeros((3,), jnp.float32)
        Wd2 = jax.random.normal(ks[3], (3 * n2, 3), dtype=jnp.float32) * scale
        bd2 = jnp.zeros((3,), jnp.float32)
        Wd3 = jax.random.normal(ks[4], (3 * n1, 3), dtype=jnp.float32) * scale
        bd3 = jnp.zeros((3,), jnp.float32)
        return {'x': x, 'Wa': Wa, 'ba': ba, 'Wd1': Wd1, 'bd1': bd1, 'Wd2': Wd2, 'bd2': bd2, 'Wd3': Wd3, 'bd3': bd3}
    _L0_tok_all = _L0_tok_setup()
    _L0_tok_in = {k: v for k, v in _L0_tok_all.items() if k in ('Wa', 'ba', 'Wd1', 'bd1', 'Wd2', 'bd2', 'Wd3', 'bd3')}
    del _L0_tok_all

    def _L0_attn_setup():
        import jax, jax.numpy as jnp
        import numpy as np
        import math
        B, T, D, M = (4, 512, 256, 64)
        key = jax.random.key(seed)
        ks = jax.random.split(key, 7)
        x = jax.random.normal(ks[0], (B, T, D), dtype=jnp.float32)
        Wk = jax.random.normal(ks[1], (M, D), dtype=jnp.float32) * math.sqrt(2.0 / M)
        Wv = jax.random.normal(ks[2], (M, D), dtype=jnp.float32) * math.sqrt(2.0 / M)
        Wq = jax.random.normal(ks[3], (M, D), dtype=jnp.float32) * math.sqrt(2.0 / M)
        Wg = jax.random.normal(ks[4], (1, D), dtype=jnp.float32) * math.sqrt(2.0 / 1)
        bg = jnp.array([1.0], dtype=jnp.float32)
        Wo = jax.random.normal(ks[5], (D, M), dtype=jnp.float32) * 0.01
        return {'x': x, 'Wk': Wk, 'Wv': Wv, 'Wq': Wq, 'Wg': Wg, 'bg': bg, 'Wo': Wo}
    _L0_attn_all = _L0_attn_setup()
    _L0_attn_in = {k: v for k, v in _L0_attn_all.items() if k in ('Wk', 'Wv', 'Wq', 'Wg', 'bg', 'Wo')}
    del _L0_attn_all

    def _L0_ffn_setup():
        import jax, jax.numpy as jnp
        import numpy as np
        DIM = 256
        HIDDEN = 512
        N_EXPERTS = 8
        TOP_K = 2
        EPS = 1e-06

        def rms_norm(x, scale, eps=EPS):
            ms = jnp.mean(jnp.square(x.astype(jnp.float32)), axis=-1, keepdims=True)
            s = scale.astype(jnp.float32) * jax.lax.rsqrt(ms + eps)
            return x * s.astype(x.dtype)

        def moe_linear(xf, ids, W):
            E = W.shape[0]
            out = jnp.zeros((xf.shape[0], W.shape[1]), dtype=xf.dtype)
            for e in range(E):
                out = out + jnp.where((ids == e)[:, None], xf @ W[e].T, 0.0)
            return out
        key = jax.random.key(seed)
        k1, k2, k3, k4 = jax.random.split(key, 4)
        x = jax.random.normal(k1, (4, 1024, DIM), dtype=jnp.float32)
        norm_scale = jnp.ones((DIM,), dtype=jnp.float32)
        w_router = jax.random.normal(k2, (N_EXPERTS, DIM), dtype=jnp.float32) / np.sqrt(DIM)
        lim_up = np.sqrt(6.0 / (DIM + 2 * HIDDEN))
        w_up = jax.random.uniform(k3, (N_EXPERTS, 2 * HIDDEN, DIM), dtype=jnp.float32, minval=-lim_up, maxval=lim_up)
        lim_dn = np.sqrt(6.0 / (HIDDEN + DIM))
        w_down = jax.random.uniform(k4, (N_EXPERTS, DIM, HIDDEN), dtype=jnp.float32, minval=-lim_dn, maxval=lim_dn)
        return {'x': x, 'norm_scale': norm_scale, 'w_router': w_router, 'w_up': w_up, 'w_down': w_down}
    _L0_ffn_all = _L0_ffn_setup()
    _L0_ffn_in = {k: v for k, v in _L0_ffn_all.items() if k in ('norm_scale', 'w_router', 'w_up', 'w_down')}
    del _L0_ffn_all

    def _L1_attn_setup():
        import jax, jax.numpy as jnp
        import numpy as np
        import math
        B, T, C = (2, 512, 256)
        H, L = (16, 64)
        DH = C // H
        DHE = DH // 2
        THETA = 10000.0

        def _rope_cache(t, dim):
            inv_freq = 1.0 / THETA ** (jnp.arange(0, dim, 2, dtype=jnp.float32) / dim)
            freqs = jnp.arange(t, dtype=jnp.float32)[:, None] * inv_freq[None, :]
            emb = jnp.concatenate((freqs, freqs), axis=-1)
            return (jnp.cos(emb), jnp.sin(emb))

        def _apply_rope(x, cos, sin):
            x1 = x[..., 0::2]
            x2 = x[..., 1::2]
            rot = jnp.stack((-x2, x1), axis=-1).reshape(x.shape)
            return x * cos[None, None] + rot * sin[None, None]
        key = jax.random.key(seed)
        ks = jax.random.split(key, 10)
        s = 0.02
        return {'x': jax.random.normal(ks[0], (B, T, C), jnp.float32), 'Wq_down': jax.random.normal(ks[1], (C, H * L), jnp.float32) * s, 'Wk_down': jax.random.normal(ks[2], (C, H * L), jnp.float32) * s, 'Wv_down': jax.random.normal(ks[3], (C, H * L), jnp.float32) * s, 'Wq_up_c': jax.random.normal(ks[4], (L, DHE), jnp.float32) * s, 'Wq_up_e': jax.random.normal(ks[5], (L, DHE), jnp.float32) * s, 'Wk_up_c': jax.random.normal(ks[6], (L, DHE), jnp.float32) * s, 'Wk_up_e': jax.random.normal(ks[7], (L, DHE), jnp.float32) * s, 'Wv_up': jax.random.normal(ks[8], (L, DH), jnp.float32) * s, 'Wc': jax.random.normal(ks[9], (C, C), jnp.float32) * s}
    _L1_attn_all = _L1_attn_setup()
    _L1_attn_in = {k: v for k, v in _L1_attn_all.items() if k in ('Wq_down', 'Wk_down', 'Wv_down', 'Wq_up_c', 'Wq_up_e', 'Wk_up_c', 'Wk_up_e', 'Wv_up', 'Wc')}
    del _L1_attn_all

    def _L1_ffn_setup():
        import jax, jax.numpy as jnp
        import numpy as np
        E = 16
        H = 256
        F = 512
        TOP_K = 1
        B, S = (2, 256)
        key = jax.random.key(seed)
        ks = jax.random.split(key, 7)
        s = 0.02
        return {'hidden_states': jax.random.normal(ks[0], (B, S, H), jnp.float32), 'w_router': jax.random.normal(ks[1], (E, H), jnp.float32) * s, 'gate_up_proj': jax.random.normal(ks[2], (E, H, 2 * F), jnp.float32) * s, 'down_proj': jax.random.normal(ks[3], (E, F, H), jnp.float32) * s, 'w_gate': jax.random.normal(ks[4], (F, H), jnp.float32) * s, 'w_up': jax.random.normal(ks[5], (F, H), jnp.float32) * s, 'w_down': jax.random.normal(ks[6], (H, F), jnp.float32) * s}
    _L1_ffn_all = _L1_ffn_setup()
    _L1_ffn_in = {k: v for k, v in _L1_ffn_all.items() if k in ('w_router', 'gate_up_proj', 'down_proj', 'w_gate', 'w_up', 'w_down')}
    del _L1_ffn_all

    def _L2_attn_setup():
        import jax, jax.numpy as jnp
        import numpy as np
        D_MODEL = 256
        D_STATE = 32
        D_CONV = 4
        EXPAND = 2
        D_INNER = EXPAND * D_MODEL
        DT_RANK = D_MODEL // 16
        BATCH = 8
        SEQ = 256

        def _silu(x):
            return x * jax.nn.sigmoid(x)

        def _layernorm(x, g, b, eps=1e-05):
            m = x.mean(-1, keepdims=True)
            v = x.var(-1, keepdims=True)
            return (x - m) / jnp.sqrt(v + eps) * g + b

        def _mamba(x, Win, convw, convb, Wx, Wdt, bdt, Alog, Dp, Wout):
            Bn, Ln, _ = x.shape
            xz = jnp.einsum('bld,ed->ble', x, Win)
            u, z = jnp.split(xz, 2, axis=-1)
            up = jnp.pad(u, ((0, 0), (D_CONV - 1, 0), (0, 0)))
            uc = convb
            for k in range(D_CONV):
                uc = uc + up[:, k:k + Ln, :] * convw[:, k]
            uc = _silu(uc)
            x_dbl = jnp.einsum('bld,ed->ble', uc, Wx)
            dt = jax.nn.softplus(jnp.einsum('blr,dr->bld', x_dbl[..., :DT_RANK], Wdt) + bdt)
            Bv = x_dbl[..., DT_RANK:DT_RANK + D_STATE]
            Cv = x_dbl[..., DT_RANK + D_STATE:]
            A = -jnp.exp(Alog)

            def step(h, ins):
                dt_t, B_t, C_t, u_t = ins
                dA = jnp.exp(dt_t[..., None] * A)
                h = dA * h + (dt_t * u_t)[..., None] * B_t[:, None, :]
                y = jnp.einsum('bdn,bn->bd', h, C_t)
                return (h, y)
            h0 = jnp.zeros((Bn, D_INNER, D_STATE), x.dtype)
            xs = (dt.transpose(1, 0, 2), Bv.transpose(1, 0, 2), Cv.transpose(1, 0, 2), uc.transpose(1, 0, 2))
            _, ys = jax.lax.scan(step, h0, xs)
            y = ys.transpose(1, 0, 2) + uc * Dp
            y = y * _silu(z)
            return jnp.einsum('bld,ed->ble', y, Wout)
        key = jax.random.key(seed)
        ks = iter(jax.random.split(key, 64))

        def rn(shape, scale):
            return jax.random.normal(next(ks), shape, jnp.float32) * scale

        def direction_params():
            return dict(Win=rn((2 * D_INNER, D_MODEL), 0.02), convw=rn((D_INNER, D_CONV), 0.1), convb=jnp.zeros((D_INNER,), jnp.float32), Wx=rn((DT_RANK + 2 * D_STATE, D_INNER), 0.02), Wdt=rn((D_INNER, DT_RANK), 0.02), bdt=rn((D_INNER,), 0.5), Alog=jnp.log(jnp.broadcast_to(jnp.arange(1, D_STATE + 1, dtype=jnp.float32), (D_INNER, D_STATE))), Dp=jnp.ones((D_INNER,), jnp.float32), Wout=rn((D_MODEL, D_INNER), 0.02), ln_g=jnp.ones((D_MODEL,), jnp.float32), ln_b=jnp.zeros((D_MODEL,), jnp.float32))
        f = direction_params()
        b = direction_params()
        inp = {'x': rn((BATCH, SEQ, D_MODEL), 1.0)}
        for k, v in f.items():
            inp[k + '_f'] = v
        for k, v in b.items():
            inp[k + '_b'] = v
        inp['Wfuse'] = rn((D_MODEL, 2 * D_MODEL), 0.02)
        inp['bfuse'] = jnp.zeros((D_MODEL,), jnp.float32)
        return inp
    _L2_attn_all = _L2_attn_setup()
    _L2_attn_in = {k: v for k, v in _L2_attn_all.items() if k in ('Win_f', 'convw_f', 'convb_f', 'Wx_f', 'Wdt_f', 'bdt_f', 'Alog_f', 'Dp_f', 'Wout_f', 'ln_g_f', 'ln_b_f', 'Win_b', 'convw_b', 'convb_b', 'Wx_b', 'Wdt_b', 'bdt_b', 'Alog_b', 'Dp_b', 'Wout_b', 'ln_g_b', 'ln_b_b', 'Wfuse', 'bfuse')}
    del _L2_attn_all

    def _L2_ffn_setup():
        import jax, jax.numpy as jnp
        import numpy as np
        TOP_K = 2
        key = jax.random.key(seed)
        ks = jax.random.split(key, 6)
        B, S, D, BN, E = (32, 512, 256, 64, 8)
        return {'x': jax.random.normal(ks[0], (B, S, D), dtype=jnp.float32), 'gate_w': jax.random.normal(ks[1], (E, D), dtype=jnp.float32) * 0.02, 'down_w': jax.random.normal(ks[2], (E, BN, D), dtype=jnp.float32) * 0.02, 'down_b': jax.random.normal(ks[3], (E, BN), dtype=jnp.float32) * 0.02, 'up_w': jax.random.normal(ks[4], (E, D, BN), dtype=jnp.float32) * 0.02, 'up_b': jax.random.normal(ks[5], (E, D), dtype=jnp.float32) * 0.02}
    _L2_ffn_all = _L2_ffn_setup()
    _L2_ffn_in = {k: v for k, v in _L2_ffn_all.items() if k in ('gate_w', 'down_w', 'down_b', 'up_w', 'up_b')}
    del _L2_ffn_all

    def _L3_attn_setup():
        import jax, jax.numpy as jnp
        import numpy as np
        import math
        DIM = 256
        HEADS = 16
        HEAD_DIM = DIM // HEADS
        SCALE = math.sqrt(HEAD_DIM)

        def _heads(y, B, T):
            return y.reshape(B, T, HEADS, HEAD_DIM).transpose(0, 2, 1, 3)
        key = jax.random.key(seed)
        ks = jax.random.split(key, 7)
        B, T, C = (2, 512, DIM)
        w = 0.02
        return {'x': jax.random.normal(ks[0], (B, T, C), dtype=jnp.float32), 'W_Q': jax.random.normal(ks[1], (C, C), dtype=jnp.float32) * w, 'W_K': jax.random.normal(ks[2], (C, C), dtype=jnp.float32) * w, 'W_V': jax.random.normal(ks[3], (C, C), dtype=jnp.float32) * w, 'W_K_prime': jax.random.normal(ks[4], (C, C), dtype=jnp.float32) * w, 'W_O': jax.random.normal(ks[5], (C, C), dtype=jnp.float32) * w, 'alpha': jnp.float32(0.5)}
    _L3_attn_all = _L3_attn_setup()
    _L3_attn_in = {k: v for k, v in _L3_attn_all.items() if k in ('W_Q', 'W_K', 'W_V', 'W_K_prime', 'W_O', 'alpha')}
    del _L3_attn_all

    def _L3_ffn_setup():
        import jax, jax.numpy as jnp
        import numpy as np
        B, K, D = (128, 32, 256)
        E = 32
        H = int(D * 0.25)

        def _rsqrt_uniform(key, shape, d):
            bound = d ** (-0.5)
            return jax.random.uniform(key, shape, jnp.float32, -bound, bound)
        key = jax.random.key(seed)
        ks = jax.random.split(key, 7)
        return {'x': jax.random.normal(ks[0], (B, K, D), jnp.float32), 'router_w': _rsqrt_uniform(ks[1], (E, D), D), 'router_b': _rsqrt_uniform(ks[2], (E,), D), 'weights1': _rsqrt_uniform(ks[3], (E, D, H), H), 'bias1': _rsqrt_uniform(ks[4], (E, H), H), 'weights2': _rsqrt_uniform(ks[5], (E, H, D), D), 'bias2': _rsqrt_uniform(ks[6], (E, D), D)}
    _L3_ffn_all = _L3_ffn_setup()
    _L3_ffn_in = {k: v for k, v in _L3_ffn_all.items() if k in ('router_w', 'router_b', 'weights1', 'bias1', 'weights2', 'bias2')}
    del _L3_ffn_all
    return {'x': x, 'cls_tok': cls_tok, 'L0_tok_Wa': _L0_tok_in['Wa'], 'L0_tok_ba': _L0_tok_in['ba'], 'L0_tok_Wd1': _L0_tok_in['Wd1'], 'L0_tok_bd1': _L0_tok_in['bd1'], 'L0_tok_Wd2': _L0_tok_in['Wd2'], 'L0_tok_bd2': _L0_tok_in['bd2'], 'L0_tok_Wd3': _L0_tok_in['Wd3'], 'L0_tok_bd3': _L0_tok_in['bd3'], 'L0_attn_Wk': _L0_attn_in['Wk'], 'L0_attn_Wv': _L0_attn_in['Wv'], 'L0_attn_Wq': _L0_attn_in['Wq'], 'L0_attn_Wg': _L0_attn_in['Wg'], 'L0_attn_bg': _L0_attn_in['bg'], 'L0_attn_Wo': _L0_attn_in['Wo'], 'L0_ffn_norm_scale': _L0_ffn_in['norm_scale'], 'L0_ffn_w_router': _L0_ffn_in['w_router'], 'L0_ffn_w_up': _L0_ffn_in['w_up'], 'L0_ffn_w_down': _L0_ffn_in['w_down'], 'L1_attn_Wq_down': _L1_attn_in['Wq_down'], 'L1_attn_Wk_down': _L1_attn_in['Wk_down'], 'L1_attn_Wv_down': _L1_attn_in['Wv_down'], 'L1_attn_Wq_up_c': _L1_attn_in['Wq_up_c'], 'L1_attn_Wq_up_e': _L1_attn_in['Wq_up_e'], 'L1_attn_Wk_up_c': _L1_attn_in['Wk_up_c'], 'L1_attn_Wk_up_e': _L1_attn_in['Wk_up_e'], 'L1_attn_Wv_up': _L1_attn_in['Wv_up'], 'L1_attn_Wc': _L1_attn_in['Wc'], 'L1_ffn_w_router': _L1_ffn_in['w_router'], 'L1_ffn_gate_up_proj': _L1_ffn_in['gate_up_proj'], 'L1_ffn_down_proj': _L1_ffn_in['down_proj'], 'L1_ffn_w_gate': _L1_ffn_in['w_gate'], 'L1_ffn_w_up': _L1_ffn_in['w_up'], 'L1_ffn_w_down': _L1_ffn_in['w_down'], 'L2_attn_Win_f': _L2_attn_in['Win_f'], 'L2_attn_convw_f': _L2_attn_in['convw_f'], 'L2_attn_convb_f': _L2_attn_in['convb_f'], 'L2_attn_Wx_f': _L2_attn_in['Wx_f'], 'L2_attn_Wdt_f': _L2_attn_in['Wdt_f'], 'L2_attn_bdt_f': _L2_attn_in['bdt_f'], 'L2_attn_Alog_f': _L2_attn_in['Alog_f'], 'L2_attn_Dp_f': _L2_attn_in['Dp_f'], 'L2_attn_Wout_f': _L2_attn_in['Wout_f'], 'L2_attn_ln_g_f': _L2_attn_in['ln_g_f'], 'L2_attn_ln_b_f': _L2_attn_in['ln_b_f'], 'L2_attn_Win_b': _L2_attn_in['Win_b'], 'L2_attn_convw_b': _L2_attn_in['convw_b'], 'L2_attn_convb_b': _L2_attn_in['convb_b'], 'L2_attn_Wx_b': _L2_attn_in['Wx_b'], 'L2_attn_Wdt_b': _L2_attn_in['Wdt_b'], 'L2_attn_bdt_b': _L2_attn_in['bdt_b'], 'L2_attn_Alog_b': _L2_attn_in['Alog_b'], 'L2_attn_Dp_b': _L2_attn_in['Dp_b'], 'L2_attn_Wout_b': _L2_attn_in['Wout_b'], 'L2_attn_ln_g_b': _L2_attn_in['ln_g_b'], 'L2_attn_ln_b_b': _L2_attn_in['ln_b_b'], 'L2_attn_Wfuse': _L2_attn_in['Wfuse'], 'L2_attn_bfuse': _L2_attn_in['bfuse'], 'L2_ffn_gate_w': _L2_ffn_in['gate_w'], 'L2_ffn_down_w': _L2_ffn_in['down_w'], 'L2_ffn_down_b': _L2_ffn_in['down_b'], 'L2_ffn_up_w': _L2_ffn_in['up_w'], 'L2_ffn_up_b': _L2_ffn_in['up_b'], 'L3_attn_W_Q': _L3_attn_in['W_Q'], 'L3_attn_W_K': _L3_attn_in['W_K'], 'L3_attn_W_V': _L3_attn_in['W_V'], 'L3_attn_W_K_prime': _L3_attn_in['W_K_prime'], 'L3_attn_W_O': _L3_attn_in['W_O'], 'L3_attn_alpha': _L3_attn_in['alpha'], 'L3_ffn_router_w': _L3_ffn_in['router_w'], 'L3_ffn_router_b': _L3_ffn_in['router_b'], 'L3_ffn_weights1': _L3_ffn_in['weights1'], 'L3_ffn_bias1': _L3_ffn_in['bias1'], 'L3_ffn_weights2': _L3_ffn_in['weights2'], 'L3_ffn_bias2': _L3_ffn_in['bias2']}

def reference(x, cls_tok, L0_tok_Wa, L0_tok_ba, L0_tok_Wd1, L0_tok_bd1, L0_tok_Wd2, L0_tok_bd2, L0_tok_Wd3, L0_tok_bd3, L0_attn_Wk, L0_attn_Wv, L0_attn_Wq, L0_attn_Wg, L0_attn_bg, L0_attn_Wo, L0_ffn_norm_scale, L0_ffn_w_router, L0_ffn_w_up, L0_ffn_w_down, L1_attn_Wq_down, L1_attn_Wk_down, L1_attn_Wv_down, L1_attn_Wq_up_c, L1_attn_Wq_up_e, L1_attn_Wk_up_c, L1_attn_Wk_up_e, L1_attn_Wv_up, L1_attn_Wc, L1_ffn_w_router, L1_ffn_gate_up_proj, L1_ffn_down_proj, L1_ffn_w_gate, L1_ffn_w_up, L1_ffn_w_down, L2_attn_Win_f, L2_attn_convw_f, L2_attn_convb_f, L2_attn_Wx_f, L2_attn_Wdt_f, L2_attn_bdt_f, L2_attn_Alog_f, L2_attn_Dp_f, L2_attn_Wout_f, L2_attn_ln_g_f, L2_attn_ln_b_f, L2_attn_Win_b, L2_attn_convw_b, L2_attn_convb_b, L2_attn_Wx_b, L2_attn_Wdt_b, L2_attn_bdt_b, L2_attn_Alog_b, L2_attn_Dp_b, L2_attn_Wout_b, L2_attn_ln_g_b, L2_attn_ln_b_b, L2_attn_Wfuse, L2_attn_bfuse, L2_ffn_gate_w, L2_ffn_down_w, L2_ffn_down_b, L2_ffn_up_w, L2_ffn_up_b, L3_attn_W_Q, L3_attn_W_K, L3_attn_W_V, L3_attn_W_K_prime, L3_attn_W_O, L3_attn_alpha, L3_ffn_router_w, L3_ffn_router_b, L3_ffn_weights1, L3_ffn_bias1, L3_ffn_weights2, L3_ffn_bias2):
    import jax
    import jax.numpy as jnp

    def _L0_tok_ref(x, Wa, ba, Wd1, bd1, Wd2, bd2, Wd3, bd3):
        import jax, jax.numpy as jnp
        import numpy as np
        INV_SQRT2 = 0.7071067811865476
        LEVEL = 3

        def _split(x, axis):
            ax = axis % x.ndim
            sl0 = [slice(None)] * x.ndim
            sl0[ax] = slice(0, None, 2)
            sl1 = [slice(None)] * x.ndim
            sl1[ax] = slice(1, None, 2)
            x0, x1 = (x[tuple(sl0)], x[tuple(sl1)])
            return ((x0 + x1) * INV_SQRT2, (x0 - x1) * INV_SQRT2)

        def _merge(lo, hi, axis):
            ax = axis % lo.ndim
            e = (lo + hi) * INV_SQRT2
            o = (lo - hi) * INV_SQRT2
            s = jnp.stack([e, o], axis=ax + 1)
            shape = list(lo.shape)
            shape[ax] *= 2
            return s.reshape(shape)

        def _dwt2(x):
            lo, hi = _split(x, -1)
            a, h = _split(lo, -2)
            v, d = _split(hi, -2)
            return (a, h, v, d)

        def _idwt2(a, h, v, d):
            lo = _merge(a, h, -2)
            hi = _merge(v, d, -2)
            return _merge(lo, hi, -1)
        img = x[..., 0]
        B = img.shape[0]
        details = []
        cur = img
        for _ in range(LEVEL):
            cur, h, v, d = _dwt2(cur)
            details.append((h, v, d))
        aw = jax.nn.sigmoid(cur.reshape(B, -1) @ Wa + ba)
        rec = cur * aw[:, :, None]
        det_params = [(Wd1, bd1), (Wd2, bd2), (Wd3, bd3)]
        for (h, v, d), (Wd, bd) in zip(reversed(details), det_params):
            flat = jnp.stack([h, v, d], axis=1).reshape(B, -1)
            w = jax.nn.softmax(flat @ Wd + bd, axis=-1)
            rec = _idwt2(rec, h * w[:, 0, None, None], v * w[:, 1, None, None], d * w[:, 2, None, None])
        return rec

    def _L0_attn_ref(x, Wk, Wv, Wq, Wg, bg, Wo):
        import jax, jax.numpy as jnp
        import numpy as np
        import math
        B, T, D, M = (4, 512, 256, 64)
        Bb, Tt, Dd = x.shape
        Mm = Wk.shape[0]
        keys = x @ Wk.T
        vals = x @ Wv.T
        queries = x @ Wq.T
        gates = jax.nn.sigmoid(x @ Wg.T + bg)
        log_gates = jnp.log(gates[..., 0] + 1e-08)
        cum_log = jnp.cumsum(log_gates, axis=1)
        log_decay = cum_log[:, None, :] - cum_log[:, :, None]
        causal = jnp.triu(jnp.ones((Tt, Tt), dtype=x.dtype))
        decay = jnp.exp(jnp.minimum(log_decay, 0.0)) * causal
        scores = jnp.einsum('bim,bjm->bij', vals, queries) / math.sqrt(Mm)
        weighted = scores * decay
        reads = jnp.einsum('bij,bim->bjm', weighted, keys) / math.sqrt(Tt)
        return reads @ Wo.T

    def _L0_ffn_ref(x, norm_scale, w_router, w_up, w_down):
        import jax, jax.numpy as jnp
        import numpy as np
        DIM = 256
        HIDDEN = 512
        N_EXPERTS = 8
        TOP_K = 2
        EPS = 1e-06

        def rms_norm(x, scale, eps=EPS):
            ms = jnp.mean(jnp.square(x.astype(jnp.float32)), axis=-1, keepdims=True)
            s = scale.astype(jnp.float32) * jax.lax.rsqrt(ms + eps)
            return x * s.astype(x.dtype)

        def moe_linear(xf, ids, W):
            E = W.shape[0]
            out = jnp.zeros((xf.shape[0], W.shape[1]), dtype=xf.dtype)
            for e in range(E):
                out = out + jnp.where((ids == e)[:, None], xf @ W[e].T, 0.0)
            return out
        B, S, D = x.shape
        skip = x
        xn = rms_norm(x, norm_scale)
        scores = (xn @ w_router.T).astype(jnp.float32)
        scores_topk, idx = jax.lax.top_k(scores, TOP_K)
        weights = jax.nn.softmax(scores_topk, axis=-1)
        xf = jnp.broadcast_to(xn[..., None, :], (B, S, TOP_K, D)).reshape(-1, D)
        ids = idx.reshape(-1)
        up = moe_linear(xf, ids, w_up)
        u, gate = jnp.split(up, 2, axis=-1)
        h = u * jax.nn.silu(gate)
        down = moe_linear(h, ids, w_down)
        down = down.reshape(B, S, TOP_K, D)
        out = jnp.sum(down * weights[..., None].astype(down.dtype), axis=-2)
        return out + skip

    def _L1_attn_ref(x, Wq_down, Wk_down, Wv_down, Wq_up_c, Wq_up_e, Wk_up_c, Wk_up_e, Wv_up, Wc):
        import jax, jax.numpy as jnp
        import numpy as np
        import math
        B, T, C = (2, 512, 256)
        H, L = (16, 64)
        DH = C // H
        DHE = DH // 2
        THETA = 10000.0

        def _rope_cache(t, dim):
            inv_freq = 1.0 / THETA ** (jnp.arange(0, dim, 2, dtype=jnp.float32) / dim)
            freqs = jnp.arange(t, dtype=jnp.float32)[:, None] * inv_freq[None, :]
            emb = jnp.concatenate((freqs, freqs), axis=-1)
            return (jnp.cos(emb), jnp.sin(emb))

        def _apply_rope(x, cos, sin):
            x1 = x[..., 0::2]
            x2 = x[..., 1::2]
            rot = jnp.stack((-x2, x1), axis=-1).reshape(x.shape)
            return x * cos[None, None] + rot * sin[None, None]
        b, t, c = x.shape
        q_lat = (x @ Wq_down).reshape(b, t, H, L)
        k_lat = (x @ Wk_down).reshape(b, t, H, L)
        v_lat = (x @ Wv_down).reshape(b, t, H, L)
        q_c = jnp.einsum('bthl,ld->bhtd', q_lat, Wq_up_c)
        q_e = jnp.einsum('bthl,ld->bhtd', q_lat, Wq_up_e)
        k_c = jnp.einsum('bthl,ld->bhtd', k_lat, Wk_up_c)
        k_e = jnp.einsum('bthl,ld->bhtd', k_lat, Wk_up_e)
        v = jnp.einsum('bthl,ld->bhtd', v_lat, Wv_up)
        cos, sin = _rope_cache(t, DHE)
        q = jnp.concatenate([q_c, _apply_rope(q_e, cos, sin)], axis=-1)
        k = jnp.concatenate([k_c, _apply_rope(k_e, cos, sin)], axis=-1)
        scale = 1.0 / math.sqrt(DH)
        scores = jnp.einsum('bhqd,bhkd->bhqk', q, k) * scale
        causal = jnp.tril(jnp.ones((t, t), dtype=bool))
        scores = jnp.where(causal[None, None], scores, -jnp.inf)
        att = jax.nn.softmax(scores, axis=-1)
        y = jnp.einsum('bhqk,bhkd->bhqd', att, v)
        y = y.transpose(0, 2, 1, 3).reshape(b, t, c)
        return y @ Wc

    def _L1_ffn_ref(hidden_states, w_router, gate_up_proj, down_proj, w_gate, w_up, w_down):
        import jax, jax.numpy as jnp
        import numpy as np
        E = 16
        H = 256
        F = 512
        TOP_K = 1
        B, S = (2, 256)
        b, s, h = hidden_states.shape
        x = hidden_states.reshape(-1, h)
        logits = x @ w_router.T
        _, top_idx = jax.lax.top_k(logits, TOP_K)
        mask = jax.nn.one_hot(top_idx, E, dtype=logits.dtype).sum(axis=1)
        scores = jax.nn.sigmoid(logits) * mask
        masked_inputs = scores.T[:, :, None] * x[None, :, :]
        gate_up = jnp.einsum('eth,ehf->etf', masked_inputs, gate_up_proj)
        gate, up = jnp.split(gate_up, 2, axis=-1)
        expert_out = jnp.einsum('etf,efh->eth', up * jax.nn.silu(gate), down_proj)
        shared = jax.nn.silu(x @ w_gate.T) * (x @ w_up.T) @ w_down.T
        out = shared + expert_out.sum(axis=0)
        return out.reshape(b, s, h)

    def _L2_attn_ref(x, Win_f, convw_f, convb_f, Wx_f, Wdt_f, bdt_f, Alog_f, Dp_f, Wout_f, ln_g_f, ln_b_f, Win_b, convw_b, convb_b, Wx_b, Wdt_b, bdt_b, Alog_b, Dp_b, Wout_b, ln_g_b, ln_b_b, Wfuse, bfuse):
        import jax, jax.numpy as jnp
        import numpy as np
        D_MODEL = 256
        D_STATE = 32
        D_CONV = 4
        EXPAND = 2
        D_INNER = EXPAND * D_MODEL
        DT_RANK = D_MODEL // 16
        BATCH = 8
        SEQ = 256

        def _silu(x):
            return x * jax.nn.sigmoid(x)

        def _layernorm(x, g, b, eps=1e-05):
            m = x.mean(-1, keepdims=True)
            v = x.var(-1, keepdims=True)
            return (x - m) / jnp.sqrt(v + eps) * g + b

        def _mamba(x, Win, convw, convb, Wx, Wdt, bdt, Alog, Dp, Wout):
            Bn, Ln, _ = x.shape
            xz = jnp.einsum('bld,ed->ble', x, Win)
            u, z = jnp.split(xz, 2, axis=-1)
            up = jnp.pad(u, ((0, 0), (D_CONV - 1, 0), (0, 0)))
            uc = convb
            for k in range(D_CONV):
                uc = uc + up[:, k:k + Ln, :] * convw[:, k]
            uc = _silu(uc)
            x_dbl = jnp.einsum('bld,ed->ble', uc, Wx)
            dt = jax.nn.softplus(jnp.einsum('blr,dr->bld', x_dbl[..., :DT_RANK], Wdt) + bdt)
            Bv = x_dbl[..., DT_RANK:DT_RANK + D_STATE]
            Cv = x_dbl[..., DT_RANK + D_STATE:]
            A = -jnp.exp(Alog)

            def step(h, ins):
                dt_t, B_t, C_t, u_t = ins
                dA = jnp.exp(dt_t[..., None] * A)
                h = dA * h + (dt_t * u_t)[..., None] * B_t[:, None, :]
                y = jnp.einsum('bdn,bn->bd', h, C_t)
                return (h, y)
            h0 = jnp.zeros((Bn, D_INNER, D_STATE), x.dtype)
            xs = (dt.transpose(1, 0, 2), Bv.transpose(1, 0, 2), Cv.transpose(1, 0, 2), uc.transpose(1, 0, 2))
            _, ys = jax.lax.scan(step, h0, xs)
            y = ys.transpose(1, 0, 2) + uc * Dp
            y = y * _silu(z)
            return jnp.einsum('bld,ed->ble', y, Wout)
        fo = _mamba(x, Win_f, convw_f, convb_f, Wx_f, Wdt_f, bdt_f, Alog_f, Dp_f, Wout_f)
        fo = _layernorm(fo, ln_g_f, ln_b_f)
        xr = x[:, ::-1, :]
        bo = _mamba(xr, Win_b, convw_b, convb_b, Wx_b, Wdt_b, bdt_b, Alog_b, Dp_b, Wout_b)
        bo = _layernorm(bo[:, ::-1, :], ln_g_b, ln_b_b)
        combined = jnp.concatenate([fo, bo], axis=-1)
        return jnp.einsum('ble,de->bld', combined, Wfuse) + bfuse

    def _L2_ffn_ref(x, gate_w, down_w, down_b, up_w, up_b):
        import jax, jax.numpy as jnp
        import numpy as np
        TOP_K = 2
        pooled = x.mean(axis=1)
        gate = jax.nn.softmax(pooled @ gate_w.T, axis=-1)
        top_w, top_i = jax.lax.top_k(gate, TOP_K)
        top_w = top_w / (top_w.sum(axis=-1, keepdims=True) + 1e-08)
        Wd = down_w[top_i]
        bd = down_b[top_i]
        Wu = up_w[top_i]
        bu = up_b[top_i]
        h = jax.nn.gelu(jnp.einsum('bsd,bkcd->bksc', x, Wd) + bd[:, :, None, :], approximate=False)
        h = h * top_w[:, :, None, None]
        out = jnp.einsum('bksc,bkdc->bsd', h, Wu)
        out = out + (top_w[:, :, None] * bu).sum(axis=1)[:, None, :]
        return out

    def _L3_attn_ref(x, W_Q, W_K, W_V, W_K_prime, W_O, alpha):
        import jax, jax.numpy as jnp
        import numpy as np
        import math
        DIM = 256
        HEADS = 16
        HEAD_DIM = DIM // HEADS
        SCALE = math.sqrt(HEAD_DIM)

        def _heads(y, B, T):
            return y.reshape(B, T, HEADS, HEAD_DIM).transpose(0, 2, 1, 3)
        B, T, C = x.shape
        q = _heads(x @ W_Q.T, B, T)
        k = _heads(x @ W_K.T, B, T)
        v = _heads(x @ W_V.T, B, T)
        kp = _heads(x @ W_K_prime.T, B, T)
        scores = jnp.einsum('bhqd,bhkd->bhqk', q, k) / SCALE
        attn = jax.nn.softmax(scores, axis=-1)
        out_std = jnp.einsum('bhqk,bhkd->bhqd', attn, v)
        scores_p = jnp.einsum('bhqd,bhkd->bhqk', q, kp) / SCALE
        attn_p = jax.nn.softmax(scores_p, axis=-1)
        out_p = jnp.einsum('bhqk,bhkd->bhqd', attn_p, v)
        out = alpha * out_std + (1.0 - alpha) * out_p
        out = out.transpose(0, 2, 1, 3).reshape(B, T, C)
        return out @ W_O.T

    def _L3_ffn_ref(x, router_w, router_b, weights1, bias1, weights2, bias2):
        import jax, jax.numpy as jnp
        import numpy as np
        B, K, D = (128, 32, 256)
        E = 32
        H = int(D * 0.25)

        def _rsqrt_uniform(key, shape, d):
            bound = d ** (-0.5)
            return jax.random.uniform(key, shape, jnp.float32, -bound, bound)
        b, k, d = x.shape
        x_flat = x.reshape(-1, d)
        n = x_flat.shape[0]
        logits = x_flat @ router_w.T + router_b
        routed_idx = jnp.argmax(logits, axis=-1)

        def expert_mlp(w1, b1, w2, b2):
            h = jax.nn.relu(x_flat @ w1 + b1)
            return jax.nn.relu(h @ w2 + b2)
        y_all = jax.vmap(expert_mlp)(weights1, bias1, weights2, bias2)
        out_flat = y_all[routed_idx, jnp.arange(n)]
        return out_flat.reshape(b, k, d)
    h = _L0_tok_ref(x, L0_tok_Wa, L0_tok_ba, L0_tok_Wd1, L0_tok_bd1, L0_tok_Wd2, L0_tok_bd2, L0_tok_Wd3, L0_tok_bd3)
    h = jnp.concatenate([jnp.broadcast_to(cls_tok, (h.shape[0], 1, h.shape[2])), h], axis=1)
    h = h + _L0_attn_ref(_layernorm(h, axis=-1), L0_attn_Wk, L0_attn_Wv, L0_attn_Wq, L0_attn_Wg, L0_attn_bg, L0_attn_Wo)
    h = h + _L0_ffn_ref(_layernorm(h, axis=-1), L0_ffn_norm_scale, L0_ffn_w_router, L0_ffn_w_up, L0_ffn_w_down)
    h = h + _L1_attn_ref(_layernorm(h, axis=-1), L1_attn_Wq_down, L1_attn_Wk_down, L1_attn_Wv_down, L1_attn_Wq_up_c, L1_attn_Wq_up_e, L1_attn_Wk_up_c, L1_attn_Wk_up_e, L1_attn_Wv_up, L1_attn_Wc)
    h = h + _L1_ffn_ref(_layernorm(h, axis=-1), L1_ffn_w_router, L1_ffn_gate_up_proj, L1_ffn_down_proj, L1_ffn_w_gate, L1_ffn_w_up, L1_ffn_w_down)
    h = h + _L2_attn_ref(_layernorm(h, axis=-1), L2_attn_Win_f, L2_attn_convw_f, L2_attn_convb_f, L2_attn_Wx_f, L2_attn_Wdt_f, L2_attn_bdt_f, L2_attn_Alog_f, L2_attn_Dp_f, L2_attn_Wout_f, L2_attn_ln_g_f, L2_attn_ln_b_f, L2_attn_Win_b, L2_attn_convw_b, L2_attn_convb_b, L2_attn_Wx_b, L2_attn_Wdt_b, L2_attn_bdt_b, L2_attn_Alog_b, L2_attn_Dp_b, L2_attn_Wout_b, L2_attn_ln_g_b, L2_attn_ln_b_b, L2_attn_Wfuse, L2_attn_bfuse)
    h = h + _L2_ffn_ref(_layernorm(h, axis=-1), L2_ffn_gate_w, L2_ffn_down_w, L2_ffn_down_b, L2_ffn_up_w, L2_ffn_up_b)
    h = h + _L3_attn_ref(_layernorm(h, axis=-1), L3_attn_W_Q, L3_attn_W_K, L3_attn_W_V, L3_attn_W_K_prime, L3_attn_W_O, L3_attn_alpha)
    h = h + _L3_ffn_ref(_layernorm(h, axis=-1), L3_ffn_router_w, L3_ffn_router_b, L3_ffn_weights1, L3_ffn_bias1, L3_ffn_weights2, L3_ffn_bias2)
    return h

_drawn_inputs = setup_inputs


def setup_inputs(seed=0):
    import zlib

    import numpy as np

    out = dict(_drawn_inputs(seed))
    spreads = {'L0_tok_bd1': (0.0, 0.281),
     'L0_tok_bd2': (0.0, 0.32),
     'L0_tok_bd3': (0.0, 0.415),
     'L0_ffn_norm_scale': (1.0, 0.2),
     'L2_attn_convb_f': (0.0, 0.1),
     'L2_attn_Dp_f': (1.0, 0.6),
     'L2_attn_ln_g_f': (1.0, 0.6),
     'L2_attn_ln_b_f': (0.0, 1.231),
     'L2_attn_convb_b': (0.0, 0.1),
     'L2_attn_Dp_b': (1.0, 0.6),
     'L2_attn_ln_g_b': (1.0, 0.6),
     'L2_attn_ln_b_b': (0.0, 0.8),
     'L2_attn_bfuse': (0.0, 0.667)}
    factors = {'L1_attn_Wq_down': 8.0,
     'L1_attn_Wk_down': 8.0,
     'L1_attn_Wv_down': 8.0,
     'L1_attn_Wq_up_c': 8.0,
     'L1_attn_Wq_up_e': 8.0,
     'L1_attn_Wk_up_c': 8.0,
     'L1_attn_Wk_up_e': 8.0,
     'L1_attn_Wv_up': 8.0,
     'L1_attn_Wc': 8.0,
     'L1_ffn_w_router': 6.04,
     'L1_ffn_gate_up_proj': 6.055,
     'L1_ffn_down_proj': 5.866,
     'L1_ffn_w_gate': 2.68,
     'L1_ffn_w_up': 2.783,
     'L1_ffn_w_down': 2.807,
     'L2_attn_Wx_f': 36.897,
     'L2_attn_Wdt_f': 64.0,
     'L2_attn_bdt_f': 30.285,
     'L2_attn_Alog_f': 64.0,
     'L2_attn_Wx_b': 59.063,
     'L2_attn_Wdt_b': 64.0,
     'L2_attn_bdt_b': 8.0,
     'L2_attn_Alog_b': 64.0,
     'L2_ffn_gate_w': 3.457,
     'L2_ffn_down_w': 3.261,
     'L2_ffn_down_b': 64.0,
     'L2_ffn_up_w': 3.244,
     'L2_ffn_up_b': 29.964,
     'L3_attn_W_Q': 8.0,
     'L3_attn_W_K': 8.0,
     'L3_attn_W_V': 5.404,
     'L3_attn_W_K_prime': 8.0,
     'L3_attn_W_O': 6.195,
     'L3_ffn_bias1': 61.502,
     'L3_ffn_bias2': 23.325,
     'L3_ffn_router_w': 3.265,
     'L3_ffn_router_b': 8.0,
     'L3_ffn_weights1': 4.402,
     'L3_ffn_weights2': 3.489}
    for name, (base, spread) in spreads.items():
        noise = np.random.default_rng([zlib.crc32(name.encode()), seed]).standard_normal(out[name].shape)
        drawn = base * np.exp(spread * noise) if base else spread * noise
        out[name] = jnp.asarray(drawn.astype(out[name].dtype))
    for name, factor in factors.items():
        out[name] = (out[name] * factor).astype(out[name].dtype)
    return out
```

```python
from contextlib import ExitStack

import numpy as np
import concourse.bass as bass
from concourse import mybir

F32 = mybir.dt.float32
BF16 = mybir.dt.bfloat16
U32 = mybir.dt.uint32
ALU = mybir.AluOpType
ACT = mybir.ActivationFunctionType
AX = mybir.AxisListType.X

P = 128
B = 8
D = 256
C = D // P
IMG = 256
T = IMG + 1
TP = 3 * P
BANK = 512
NEG = -1.0e30


class Turn:

    def __init__(self, i, per, credit=0):
        self.i, self.per, self.credit = i, per, credit

    def __call__(self, n):
        return self.i * self.per + (n + self.credit)


def signal(nc, ctx, name):
    return ctx.enter_context(nc.semaphore(name))


class Link:

    def __init__(self, eng, sem):
        self.eng, self.sem, self.i, self.per, self.k, self.done = eng, sem, None, 0, 0, 0

    def __call__(self, ins):
        ins.then_inc(self.sem, 1)
        self.k += 1
        at = self.done + self.k
        self.eng.wait_ge(self.sem, at if self.i is None else self.i * self.per + at)

    def enter(self, i, per):
        self.done, self.k, self.i, self.per = self.done + self.k, 0, i, per

    def leave(self, rounds):
        assert self.k == self.per, (self.k, self.per)
        self.done, self.k, self.i = self.done + rounds * self.per, 0, None


def settle(eng, k):
    eng.sem_inc(k.passed, 1)


def clear(nc, k, sems):
    with nc.Block() as block:
        @block.vector
        def _(dve):
            for sem in [*sems, *k.shared]:
                dve.sem_clear(sem)


class Kit:
    pass


def section_constants(nc, k, cls_tok):
    with nc.Block() as block:
        @block.sync
        def _(sp):
            sp.dma_start(k.cls[:], cls_tok).then_inc(k.loads, 16)
            sp.wait_ge(k.loads, 16)

        @block.vector
        def _(dve):
            nc.vector.memset(k.ones[:], 1.0)
            nc.vector.memset(k.mean[:], 1.0 / D)
            nc.vector.memset(k.eps[:, 0:1], 1e-5)
            nc.vector.memset(k.eps[:, 1:2], 1e-6)
            nc.vector.memset(k.xb[:], 0.0)
            nc.vector.memset(k.ident[:], 0.0).then_inc(k.const_set, 1)

        @block.gpsimd
        def _(pool):
            pool.wait_ge(k.const_set, 1)
            nc.gpsimd.affine_select(out=k.ident[:], in_=k.ident[:], compare_op=ALU.not_equal, fill=1.0,
                                    base=0, pattern=[[-1, P]], channel_multiplier=1).then_inc(k.const_set, 1)
            pool.wait_ge(k.const_set, 2)


def section_tokens(nc, k, img, wa, wd, tok_b):
    rows = [IMG >> l for l in range(4)]
    cols = [8 >> l for l in range(4)]
    BB = 2
    G = 32
    with ExitStack() as ctx:
        sb = lambda name, shape: ctx.enter_context(nc.sbuf_tensor("tok_" + name, shape, F32))
        pix = sb("pix", [P, BB, cols[0], rows[0]])
        lo = sb("lo", [P, BB, cols[1], rows[0]])
        hi = sb("hi", [P, BB, cols[1], rows[0]])
        low = [None] + [sb(f"low{l}", [P, BB, cols[l], rows[l]]) for l in (1, 2, 3)]
        det = [None] + [sb(f"det{l}", [P, BB, 3, cols[l], rows[l]]) for l in (1, 2, 3)]
        w = [None] + [sb(f"w{l}", [P, 3, 3 * cols[l] * rows[l]]) for l in (1, 2, 3)]
        wca = sb("wca", [P, rows[3]])
        prod = sb("prod", [P, 3 * cols[1] * rows[1]])
        group = sb("group", [P, P])
        bias = sb("bias", [P, 10])
        part = sb("part", [P, 20])
        lg = sb("lg", [P, 20])
        ex = sb("ex", [P, 20])
        mx = sb("mx", [P, 6])
        den = sb("den", [P, 6])
        sums = ctx.enter_context(nc.psum_tensor("tok_sums", [P, BANK], F32))
        back = nc.dram_tensor("tok_back", [B, D, IMG], F32).ap()
        back_out = back.rearrange("(s b) (q r) n -> s (b q) (r n)", s=BB, r=cols[0])
        back_in = back.rearrange("b (c f) n -> c f b n", c=C)
        sigs = img_in, w_in, dots, summed, logits, exped, rec_done, out_done, tok_in = tuple(
            signal(nc, ctx, "tok_" + n) for n in ("img_in", "w_in", "dots", "summed", "logits", "exped", "rec_done", "out_done", "tok_in"))

        with nc.Block() as block:
            @block.sync
            def _(sp):
                sp.dma_start(pix[:], img).then_inc(img_in, 16)
                for g in range(4):
                    for l in (1, 2, 3):
                        sp.dma_start(w[l][G * g:G * g + G], wd[l]).then_inc(w_in, 16)
                    sp.dma_start(wca[G * g:G * g + G], wa).then_inc(w_in, 16)
                sp.dma_start(bias[:], tok_b.partition_broadcast(P)).then_inc(w_in, 16)
                for bb in range(BB):
                    sp.wait_ge(rec_done, bb + 1)
                    sp.dma_start(back_out[bb], pix[:, bb].rearrange("p r n -> p (r n)")).then_inc(out_done, 16)
                sp.wait_ge(out_done, 16 * BB)
                for c in range(C):
                    sp.dma_start(k.h[:, c, :, 1:T], back_in[c]).then_inc(tok_in, 16)
                sp.wait_ge(tok_in, 16 * C)

            @block.tensor
            def _(pe):
                pe.wait_ge(dots, 1)
                nc.tensor.matmul(sums[:, 0:20], group[:], part[:], start=True, stop=True).then_inc(summed, 1)

            @block.scalar
            def _(act):
                act.wait_ge(logits, 1)
                nc.scalar.activation(ex[:], lg[:], ACT.Exp).then_inc(exped, 1)

            @block.vector
            def _(dve):
                link = Link(dve, k.dve_link)
                for c in range(C):
                    nc.vector.tensor_copy(k.h[:, c, :, 0], k.cls[:, c:c + 1].broadcast_to([P, B]))
                nc.vector.memset(group[:], 0.0)
                link(nc.vector.memset(part[:], 0.0))
                for g in range(4):
                    nc.vector.memset(group[G * g:G * g + G, G * g:G * g + G], 1.0)
                dve.wait_ge(img_in, 16)
                link(nc.vector.tensor_scalar_mul(pix[:], pix[:], 0.5))
                src = pix
                for l in (1, 2, 3):
                    R, N = cols[l], rows[l]
                    L, Hh = lo[:, :, 0:R, 0:2 * N], hi[:, :, 0:R, 0:2 * N]
                    nc.vector.tensor_tensor(L, src[:, :, 0::2, :], src[:, :, 1::2, :], ALU.add)
                    link(nc.vector.tensor_tensor(Hh, src[:, :, 0::2, :], src[:, :, 1::2, :], ALU.subtract))
                    for bb in range(BB):
                        L0, L1 = lo[:, bb, 0:R, 0:2 * N:2], lo[:, bb, 0:R, 1:2 * N:2]
                        H0, H1 = hi[:, bb, 0:R, 0:2 * N:2], hi[:, bb, 0:R, 1:2 * N:2]
                        nc.vector.tensor_tensor(low[l][:, bb], L0, L1, ALU.add)
                        nc.vector.tensor_tensor(det[l][:, bb, 0], L0, L1, ALU.subtract)
                        nc.vector.tensor_tensor(det[l][:, bb, 1], H0, H1, ALU.add)
                        last = nc.vector.tensor_tensor(det[l][:, bb, 2], H0, H1, ALU.subtract)
                    link(last)
                    if l < 3:
                        link(nc.vector.tensor_scalar_mul(low[l][:], low[l][:], 0.5))
                    src = low[l]
                dve.wait_ge(w_in, 16 * 17)
                for j, l in enumerate((3, 2, 1)):
                    n = 3 * cols[l] * rows[l]
                    for bb in range(BB):
                        for s in range(3):
                            at = j * 6 + bb * 3 + s
                            link(nc.vector.tensor_tensor_reduce(
                                prod[:, 0:n], det[l][:, bb].rearrange("p s r n -> p (s r n)"), w[l][:, s], 1.0, 0.0,
                                ALU.mult, ALU.add, part[:, at:at + 1]))
                for bb in range(BB):
                    ins = nc.vector.tensor_tensor_reduce(prod[:, 0:rows[3]], low[3][:, bb, 0], wca[:], 1.0, 0.0,
                                                         ALU.mult, ALU.add, part[:, 18 + bb:19 + bb])
                    if bb == 0:
                        link(ins)
                ins.then_inc(dots, 1)
                dve.wait_ge(summed, 1)
                nc.vector.tensor_tensor(lg[:, 0:18].rearrange("p (l b s) -> p l b s", b=BB, s=3),
                                        sums[:, 0:18].rearrange("p (l b s) -> p l b s", b=BB, s=3),
                                        bias[:, 0:9].rearrange("p (l s) -> p l s", s=3).unsqueeze(2).broadcast_to([P, 3, BB, 3]),
                                        ALU.add)
                link(nc.vector.tensor_scalar(lg[:, 18:20], sums[:, 18:20], bias[:, 9:10], -1.0, ALU.add, ALU.mult))
                lg3 = lg[:, 0:18].rearrange("p (g s) -> p g s", s=3)
                ex3 = ex[:, 0:18].rearrange("p (g s) -> p g s", s=3)
                link(nc.vector.tensor_reduce(mx[:], lg3, AX, ALU.max))
                nc.vector.tensor_tensor(lg3, lg3, mx[:].unsqueeze(2).broadcast_to([P, 6, 3]), ALU.subtract).then_inc(logits, 1)
                dve.wait_ge(exped, 1)
                nc.vector.tensor_scalar(ex[:, 18:20], ex[:, 18:20], 1.0, None, ALU.add)
                link(nc.vector.tensor_reduce(den[:], ex3, AX, ALU.add))
                nc.vector.reciprocal(ex[:, 18:20], ex[:, 18:20])
                link(nc.vector.reciprocal(den[:], den[:]))
                link(nc.vector.tensor_tensor(ex3, ex3, den[:].unsqueeze(2).broadcast_to([P, 6, 3]), ALU.mult))
                link(nc.vector.tensor_scalar_mul(ex[:], ex[:], 0.5))
                for bb in range(BB):
                    nc.vector.tensor_scalar_mul(low[3][:, bb], low[3][:, bb], ex[:, 18 + bb:19 + bb])
                    for j, l in enumerate((3, 2, 1)):
                        for s in range(3):
                            at = j * 6 + bb * 3 + s
                            last = nc.vector.tensor_scalar_mul(det[l][:, bb, s], det[l][:, bb, s], ex[:, at:at + 1])
                link(last)
                for l in (3, 2, 1):
                    R, N = cols[l], rows[l]
                    for bb in range(BB):
                        L0, L1 = lo[:, bb, 0:R, 0:2 * N:2], lo[:, bb, 0:R, 1:2 * N:2]
                        H0, H1 = hi[:, bb, 0:R, 0:2 * N:2], hi[:, bb, 0:R, 1:2 * N:2]
                        nc.vector.tensor_tensor(L0, low[l][:, bb], det[l][:, bb, 0], ALU.add)
                        nc.vector.tensor_tensor(L1, low[l][:, bb], det[l][:, bb, 0], ALU.subtract)
                        nc.vector.tensor_tensor(H0, det[l][:, bb, 1], det[l][:, bb, 2], ALU.add)
                        last = nc.vector.tensor_tensor(H1, det[l][:, bb, 1], det[l][:, bb, 2], ALU.subtract)
                    link(last)
                    dst = low[l - 1] if l > 1 else pix
                    for bb in range(BB):
                        L, Hh = lo[:, bb, 0:R, 0:2 * N], hi[:, bb, 0:R, 0:2 * N]
                        nc.vector.tensor_tensor(dst[:, bb, 0::2, :], L, Hh, ALU.add)
                        last = nc.vector.tensor_tensor(dst[:, bb, 1::2, :], L, Hh, ALU.subtract)
                        if l == 1:
                            last.then_inc(rec_done, 1)
                    if l > 1:
                        link(last)
                        link(nc.vector.tensor_scalar_mul(dst[:], dst[:], 0.5))
        clear(nc, k, sigs)


def layer_norm(nc, k, block, after=None):
    cen, sq, rstd, ps = k.ln_cen, k.ln_sq, k.ln_rstd, k.ln_ps

    def tensor(pe):
        with pe.Fori(0, B) as i:
            pe.wait_ge(k.ln_free, i + 1)
            for c in range(C):
                ins = nc.tensor.matmul(ps[:, 0, 0:T], k.mean[:], k.h[:, c, bass.ds(i, 1), :], start=(c == 0), stop=(c == C - 1))
            ins.then_inc(k.ln_mean, 1)
            pe.wait_ge(k.ln_sqd, i + 1)
            for c in range(C):
                ins = nc.tensor.matmul(ps[:, 1, 0:T], k.mean[:], sq[:, c, :], start=(c == 0), stop=(c == C - 1))
            ins.then_inc(k.ln_var, 1)

    def scalar(act):
        act.preload_act_table_set("natural_log_exp_and_others")
        with act.Fori(0, B) as i:
            act.wait_ge(k.ln_cent, i + 1)
            nc.scalar.activation(sq[:], cen[:], ACT.Square).then_inc(k.ln_sqd, 1)
            act.wait_ge(k.ln_var, i + 1)
            nc.scalar.activation(rstd[:], ps[:, 1, 0:T], ACT.Ln, bias=k.eps[:, 0:1]).then_inc(k.ln_log, 1)
            act.wait_ge(k.ln_log, i + 1)
            nc.scalar.activation(rstd[:], rstd[:], ACT.Exp, scale=-0.5).then_inc(k.ln_std, 1)

    def vector(dve):
        dve.sem_inc(k.ln_free, 1)
        with dve.Fori(0, B) as i:
            dve.wait_ge(k.ln_mean, i + 1)
            hb = k.h[:, :, bass.ds(i, 1), :].rearrange("p c o t -> p c (o t)")
            nc.vector.tensor_tensor(cen[:], hb, ps[:, 0, 0:T].unsqueeze(1).broadcast_to([P, C, T]), ALU.subtract).then_inc(k.ln_cent, 1)
            dve.wait_ge(k.ln_std, i + 1)
            xo = k.x[:, :, bass.ds(i, 1), :].rearrange("p c o t -> p c (o t)")
            nc.vector.tensor_tensor(xo, cen[:], rstd[:].unsqueeze(1).broadcast_to([P, C, T]), ALU.mult).then_inc(k.ln_free, 1)

    return tensor, scalar, vector


def section_memory(nc, k, wqv, wk, wg, bg, wo):
    M = 64
    SC = 1.0 / (M ** 0.5) / (T ** 0.5)
    with ExitStack() as ctx:
        sb = lambda name, shape: ctx.enter_context(nc.sbuf_tensor("mem_" + name, shape, F32))
        ps = lambda name, shape: ctx.enter_context(nc.psum_tensor("mem_" + name, shape, F32))
        w_qv, w_k = sb("wqv", [P, C, 2 * M]), sb("wk", [P, C, M])
        w_g, w_gb = sb("wg", [P, C]), sb("wgb", [P, C, P])
        w_o, nbg = sb("wo", [M, D]), sb("nbg", [P, 1])
        mask = sb("mask", [P, T])
        q_t, v_t = sb("q", [M, T]), sb("v", [M, T])
        keys = sb("keys", [P, 3, M])
        gate, cum, ccol = sb("gate", [P, T]), sb("cum", [P, T]), sb("ccol", [P, 2])
        dec = sb("dec", [P, 2, T])
        wei = sb("wei", [P, 3, T])
        reads = sb("reads", [M, T])
        p_v, p_qo, p_g, p_s = ps("pv", [P, BANK]), ps("pqo", [P, 2, BANK]), ps("pg", [P, BANK]), ps("ps", [P, BANK])
        p_r = ps("pr", [P, BANK])
        p_k = k.ln_ps[:, 0, :]
        p_s1 = k.ln_ps[:, 1, :]
        names = "w_in w_ready mask_set x_in proj qv_out keys_out gate_pre exp_gate gate_one log_gate cols decays scored weighed readed reads_out outed".split()
        s = {n: signal(nc, ctx, "mem_" + n) for n in names}
        ln_tensor, ln_scalar, ln_vector = layer_norm(nc, k, None)
        with nc.Block() as block:
            @block.sync
            def _(sp):
                for dst, src in ((w_qv[:], wqv), (w_k[:], wk), (w_g[:], wg), (w_o[:], wo), (nbg[:], bg.partition_broadcast(P))):
                    sp.dma_start(dst, src).then_inc(s["w_in"], 16)

            @block.gpsimd
            def _(pool):
                nc.gpsimd.memset(mask[:], SC).then_inc(s["mask_set"], 1)
                pool.wait_ge(s["mask_set"], 1)
                nc.gpsimd.affine_select(out=mask[:], in_=mask[:], compare_op=ALU.is_ge, fill=0.0, base=0,
                                        pattern=[[1, T]], channel_multiplier=-1).then_inc(s["mask_set"], 1)
                with pool.Fori(0, B) as i:
                    pool.wait_ge(k.ln_free, i + 2)
                    pool.wait_ge(s["keys_out"], i + 1)
                    nc.gpsimd.tensor_copy(k.xb[:, :, 0:T], k.x[:, :, bass.ds(i, 1), :].rearrange("p c o t -> p c (o t)")).then_inc(s["x_in"], 1)

            @block.tensor
            def _(pe):
                ln_tensor(pe)
                pe.wait_ge(s["w_ready"], 1)
                pe.wait_ge(k.ln_free, B + 1)
                pe.wait_ge(s["w_in"], 16 * 5)
                with pe.Fori(0, B) as i:
                    pe.wait_ge(s["x_in"], i + 1)
                    pe.wait_ge(s["outed"], i + 1)
                    for c in range(C):
                        nc.tensor.matmul(p_g[:, 0:T], w_gb[:, c, :], k.xb[:, c, 0:T], start=(c == 0), stop=(c == C - 1))
                    for c in range(C):
                        nc.tensor.matmul(p_qo[0:M, 0, 0:T], w_qv[:, c, 0:M], k.xb[:, c, 0:T], start=(c == 0), stop=(c == C - 1))
                    for c in range(C):
                        nc.tensor.matmul(p_v[0:M, 0:T], w_qv[:, c, M:2 * M], k.xb[:, c, 0:T], start=(c == 0), stop=(c == C - 1))
                    for t in range(3):
                        for c in range(C):
                            ins = nc.tensor.matmul(p_k[:, t * M:t * M + M], k.xb[:, c, t * P:t * P + P], w_k[:, c, :], start=(c == 0), stop=(c == C - 1))
                    ins.then_inc(s["proj"], 1)
                    pe.wait_ge(s["qv_out"], i + 1)
                    nc.tensor.matmul(p_s[:, 0:T], v_t[:, 0:P], q_t[:], start=True, stop=True)
                    nc.tensor.matmul(p_s1[:, 0:T - P], v_t[:, P:2 * P], q_t[:, P:T], start=True, stop=True)
                    nc.tensor.matmul(p_s1[0:1, 256:257], v_t[:, 2 * P:T], q_t[:, 2 * P:T], start=True, stop=True).then_inc(s["scored"], 1)
                    pe.wait_ge(s["weighed"], i + 1)
                    pe.wait_ge(s["keys_out"], i + 2)
                    nc.tensor.matmul(p_r[0:M, 0:T], keys[:, 0, :], wei[:, 0, :], start=True, stop=False)
                    nc.tensor.matmul(p_r[0:M, 0:T], keys[:, 1, :], wei[:, 1, :], start=False, stop=False)
                    nc.tensor.matmul(p_r[0:M, 0:T], keys[0:1, 2, :], wei[0:1, 2, :], start=False, stop=True).then_inc(s["readed"], 1)
                    pe.wait_ge(s["reads_out"], i + 1)
                    for c in range(C):
                        ins = nc.tensor.matmul(p_qo[:, c, 0:T], w_o[:, c * P:c * P + P], reads[:], start=True, stop=True)
                    ins.then_inc(k.ffn_out, 1)

            @block.scalar
            def _(act):
                ln_scalar(act)
                act.preload_act_table_set("natural_log_exp_and_others")
                link = Link(act, k.act_link)
                with act.Fori(0, B) as i:
                    act.wait_ge(s["proj"], i + 1)
                    nc.scalar.activation(gate[:], p_g[:, 0:T], ACT.Exp, bias=nbg[:], scale=-1.0).then_inc(s["exp_gate"], 1)
                    nc.scalar.copy(q_t[:], p_qo[0:M, 0, 0:T])
                    nc.scalar.copy(v_t[:], p_v[0:M, 0:T]).then_inc(s["qv_out"], 1)
                    act.wait_ge(s["gate_one"], i + 1)
                    nc.scalar.activation(gate[:], gate[:], ACT.Ln).then_inc(s["log_gate"], 1)
                    act.wait_ge(s["cols"], i + 1)
                    nc.scalar.activation(dec[:, 0, :], dec[:, 0, :], ACT.Exp)
                    nc.scalar.activation(dec[:, 1, P:T], dec[:, 1, P:T], ACT.Exp).then_inc(s["decays"], 1)
                    act.wait_ge(s["readed"], i + 1)
                    nc.scalar.copy(reads[:], p_r[0:M, 0:T]).then_inc(s["reads_out"], 1)

            @block.vector
            def _(dve):
                link = Link(dve, k.dve_link)
                dve.wait_ge(s["w_in"], 16 * 5)
                link(nc.vector.tensor_scalar_mul(nbg[:], nbg[:], -1.0))
                nc.vector.memset(wei[:], 0.0)
                link(nc.vector.tensor_copy(w_gb[:], w_g[:].unsqueeze(2).broadcast_to([P, C, P])))
                nc.vector.memset(keys[:], 0.0).then_inc(s["w_ready"], 1)
                dve.sem_inc(s["keys_out"], 1)
                dve.sem_inc(s["outed"], 1)
                ln_vector(dve)
                dve.wait_ge(s["mask_set"], 2)
                with dve.Fori(0, B) as i:
                    link.enter(i, 7)
                    dve.wait_ge(s["proj"], i + 1)
                    nc.vector.tensor_copy(keys[:], p_k[:, 0:3 * M].rearrange("p (t m) -> p t m", t=3)).then_inc(s["keys_out"], 1)
                    dve.wait_ge(s["exp_gate"], i + 1)
                    link(nc.vector.tensor_scalar_add(gate[:], gate[:], 1.0))
                    link(nc.vector.reciprocal(gate[:], gate[:]))
                    nc.vector.tensor_scalar_add(gate[:], gate[:], 1e-8).then_inc(s["gate_one"], 1)
                    dve.wait_ge(s["log_gate"], i + 1)
                    link(nc.vector.tensor_tensor_scan(cum[:], k.ones[:, 0:T], gate[:], 0.0, ALU.mult, ALU.add))
                    for t in range(2):
                        link(nc.vector.tensor_tensor_reduce(k.junk[:, 0:P], cum[:, t * P:t * P + P], k.ident[:], 1.0, 0.0,
                                                            ALU.mult, ALU.add, ccol[:, t:t + 1]))
                    nc.vector.tensor_scalar(dec[:, 0, 0:T], cum[:, 0:T], ccol[:, 0:1], 0.0, ALU.subtract, ALU.min)
                    nc.vector.tensor_scalar(dec[:, 1, P:T], cum[:, P:T], ccol[:, 1:2], 0.0, ALU.subtract, ALU.min).then_inc(s["cols"], 1)
                    dve.wait_ge(s["scored"], i + 1)
                    nc.vector.tensor_tensor(wei[:, 0, :], p_s[:, 0:T], mask[:], ALU.mult)
                    nc.vector.tensor_tensor(wei[0:1, 2, 256:257], p_s1[0:1, 256:257], mask[0:1, 0:1], ALU.mult)
                    link(nc.vector.tensor_tensor(wei[:, 1, P:T], p_s1[:, 0:T - P], mask[:, 0:T - P], ALU.mult))
                    dve.wait_ge(s["decays"], i + 1)
                    link(nc.vector.tensor_tensor(wei[:, 0, :], wei[:, 0, :], dec[:, 0, :], ALU.mult))
                    nc.vector.tensor_tensor(wei[:, 1, P:T], wei[:, 1, P:T], dec[:, 1, P:T], ALU.mult).then_inc(s["weighed"], 1)
                    dve.wait_ge(k.ffn_out, i + 1)
                    hb = k.h[:, :, bass.ds(i, 1), :].rearrange("p c o t -> p c (o t)")
                    nc.vector.tensor_tensor(hb, hb, p_qo[:, :, 0:T], ALU.add).then_inc(s["outed"], 1)
                link.leave(B)
        clear(nc, k, s.values())


HEADS, DH, G, J4 = 16, 16, 4, 4
TL = TP - P + 32


def section_attention(nc, k, tag, causal, scale, con, w_q, w_k, w_v, w_o, fold=None, rope=None, w_k2=None, alpha=None):
    A = 2 if w_k2 is not None else 1
    NQ = 2 + (A - 1)
    with ExitStack() as ctx:
        sb = lambda name, shape, dt=F32: ctx.enter_context(nc.sbuf_tensor(tag + "_" + name, shape, dt))
        ps = lambda name, shape: ctx.enter_context(nc.psum_tensor(tag + "_" + name, shape, F32))
        NR = 2 if rope else 1
        wqk = sb("wqk", [P, NQ, NR, C, G * P])
        wv = sb("wv", [P, C, D])
        wo = sb("wo", [P, G, D])
        qk = sb("qk", [P, NQ, G, TL])
        va = sb("va", [P, 2, HEADS, 32])
        vl = sb("vl", [P, HEADS, 32])
        xl = sb("xl", [P, C, P])
        mp = sb("mp", [P, 2, G, P])
        ml = sb("ml", [P, A, G])
        pe_p = sb("p", [P, 2, 2, T])
        pl = sb("pl", [P, 2, T])
        os_ = sb("os", [P, 2, T])
        rc = sb("rc", [P, T])
        og = sb("og", [P, G, T])
        t1 = sb("t1", [P, T])
        cst = sb("cst", [P, 6, P])
        ind = sb("ind", [P, 2])
        al = sb("al", [P, 2])
        rp = sb("rp", [P, 2, T]) if rope else None
        pa = ps("pa", [P, 2, 2, BANK])
        px = ps("px", [P, BANK])
        po = ps("po", [P, BANK])
        NEGI, SH, SEL, MQ, MK = 0, 1, 3, 4, 5
        names = "w_in w_ready x_in x_free pa_done pa_free px_done px_free qk_set exp_done pl_done o_done o_free r_done og_done y_done fold_done fold_out".split()
        s = {n: signal(nc, ctx, tag + "_" + n) for n in names}
        ln_tensor, ln_scalar, ln_vector = layer_norm(nc, k, None)
        NU = G * NQ + 2
        NS = HEADS * A
        NT = NU + 2 * NS
        NX = G * A + G + G * A
        n_in = 6 + (0 if fold else 1 + (A - 1)) + (1 if rope else 0) + (1 if alpha is not None else 0) + (6 if fold else 1)

        if fold:
            fd = sb("fd", [64, 3, HEADS, D])
            fu = sb("fu", [64, 2 * 64 + DH])

        with nc.Block() as block:
            @block.sync
            def _(sp):
                ld = lambda dst, src: sp.dma_start(dst, src).then_inc(s["w_in"], 16)
                n = 0
                if fold:
                    for j in range(3):
                        ld(fd[:, j], fold[j]); n += 1
                    ld(fu[:], fold[3]); n += 1
                else:
                    ld(wqk[:, 0, 0], w_q); ld(wqk[:, 1, 0], w_k); ld(wv[:], w_v); n += 3
                    if A == 2:
                        ld(wqk[:, 2, 0], w_k2); n += 1
                ld(wo[:], w_o); ld(cst[:], con["cst"]); ld(ind[:], con["ind"]); n += 3
                if rope:
                    ld(rp[:], rope); n += 1
                if alpha is not None:
                    ld(al[:, 0:1], alpha.partition_broadcast(P)); n += 1
                sp.wait_ge(s["w_in"], 16 * n)
                sp.sem_inc(s["w_ready"], 1)

            @block.gpsimd
            def _(pool):
                pool.wait_ge(k.ln_free, B + 1)
                with pool.Fori(0, B) as i:
                    pool.wait_ge(s["x_free"], i + 1)
                    nc.gpsimd.tensor_copy(k.xb[:, :, 0:T], k.x[:, :, bass.ds(i, 1), :].rearrange("p c o t -> p c (o t)"))
                    nc.gpsimd.tensor_copy(xl[:], k.x[:, :, bass.ds(i, 1), T - 1:T].rearrange("p c o t -> p c (o t)").broadcast_to([P, C, P])).then_inc(s["x_in"], 1)

            @block.tensor
            def _(pe):
                ln_tensor(pe)
                pe.wait_ge(s["w_ready"], 1)
                pe.wait_ge(k.ln_free, B + 1)
                if fold:
                    for m in range(3):
                        for c in range(C):
                            n = m * C + c
                            pe.wait_ge(s["fold_out"], n + 1)
                            for h in range(HEADS):
                                wide = 64 if m < 2 else DH
                                dst = pa[:, h // 8, 0, (h % 8) * 64:(h % 8) * 64 + wide]
                                ins = nc.tensor.matmul(dst, fd[:, m, h, c * P:c * P + P], fu[:, m * 64:m * 64 + wide], start=True, stop=True)
                            ins.then_inc(s["fold_done"], 1)
                pe.wait_ge(s["fold_out"], 7)
                with pe.Fori(0, B) as i:
                    pa_free, pa_done = Turn(i, NT, 2), Turn(i, NT)
                    px_free, px_done = Turn(i, NX, 1), Turn(i, NX)
                    o_free, o_done = Turn(i, G * A, 1), Turn(i, G * A)
                    r_done, og_done = Turn(i, G * A), Turn(i, G * A + 1, 1)
                    exp_done = Turn(i, NS)
                    pe.wait_ge(s["x_in"], i + 1)
                    pe.wait_ge(s["pa_free"], pa_free(0))
                    n = 0
                    for g in range(G):
                        for m in range(NQ):
                            pe.wait_ge(s["pa_free"], pa_free(n - 1))
                            for r in range(NR):
                                for c in range(C):
                                    ins = nc.tensor.matmul(pa[:, n % 2, r, 0:T], wqk[:, m, r, c, g * P:g * P + P], k.xb[:, c, 0:T], start=(c == 0), stop=(c == C - 1))
                            ins.then_inc(s["pa_done"], 1)
                            n += 1
                    pe.wait_ge(s["pa_free"], pa_free(n - 1))
                    for t in range(2):
                        for c in range(C):
                            ins = nc.tensor.matmul(pa[:, n % 2, t, 0:D], k.xb[:, c, t * P:t * P + P], wv[:, c, :], start=(c == 0), stop=(c == C - 1))
                    ins.then_inc(s["pa_done"], 1)
                    n += 1
                    pe.wait_ge(s["pa_free"], pa_free(n - 1))
                    for c in range(C):
                        ins = nc.tensor.matmul(pa[:, n % 2, 0, 0:D], xl[:, c, :], wv[:, c, :], start=(c == 0), stop=(c == C - 1))
                    ins.then_inc(s["pa_done"], 1)
                    n += 1
                    pe.wait_ge(s["pa_free"], pa_free(n))
                    x = 0
                    for a in range(A):
                        for g in range(G):
                            pe.wait_ge(s["px_free"], px_free(x))
                            settle(pe, k)
                            for j in range(J4):
                                r = slice(32 * j, 32 * j + 32)
                                ins = nc.tensor.matmul(px[r, 0:T], qk[r, 0, g, 256:288], qk[r, 1 + a, g, 0:T], start=True, stop=True)
                            ins.then_inc(s["px_done"], 1)
                            x += 1
                            for j in range(J4):
                                r = slice(32 * j, 32 * j + 32)
                                pe.wait_ge(s["pa_free"], pa_free(n - 1))
                                for t in range(2):
                                    w = (t + 1) * P if causal else T
                                    ins = nc.tensor.matmul(pa[:, n % 2, t, 0:w], qk[r, 0, g, t * P:t * P + P], qk[r, 1 + a, g, 0:w], start=True, stop=not causal)
                                    if causal:
                                        ins = nc.tensor.matmul(pa[:, n % 2, t, t * P:w], k.ident[:], cst[:, MQ, :], start=False, stop=True)
                                ins.then_inc(s["pa_done"], 1)
                                n += 1
                    pe.wait_ge(s["pa_free"], pa_free(n))
                    for g in range(G):
                        pe.wait_ge(s["px_free"], px_free(x))
                        for t in range(2):
                            nc.tensor.matmul(px[:, t * P:t * P + P], mp[:, t, g, :], cst[:, NEGI, :], start=True, stop=True)
                        for a in range(A):
                            ins = nc.tensor.matmul(px[:, 256:257], cst[:, SH + a, :], ml[:, a, g:g + 1], start=(a == 0), stop=(a == A - 1))
                        ins.then_inc(s["px_done"], 1)
                        x += 1
                    pe.wait_ge(s["qk_set"], i + 1)
                    heads = [(a, g, j) for a in range(A) for g in range(G) for j in range(J4)]

                    def values(h):
                        a, g, j = heads[h]
                        r = slice(32 * j, 32 * j + 32)
                        if j == 0:
                            pe.wait_ge(s["o_free"], o_free(a * G + g))
                        pe.wait_ge(s["exp_done"], exp_done(h + 1))
                        hd = g * J4 + j
                        nc.tensor.matmul(po[r, 0:T], va[:, 0, hd, :], pe_p[:, h % 2, 0, :], start=True, stop=False)
                        q0 = P if causal else 0
                        nc.tensor.matmul(po[r, q0:T], va[:, 1, hd, :], pe_p[:, h % 2, 1, q0:T], start=False, stop=False)
                        q0 = T - 1 if causal else 0
                        ins = nc.tensor.matmul(po[r, q0:T], vl[32 * j:32 * j + 1, hd, :], pl[32 * j:32 * j + 1, g % 2, q0:T], start=False, stop=True)
                        if j == J4 - 1:
                            ins.then_inc(s["o_done"], 1)

                    def denominators(n):
                        pe.wait_ge(s["o_free"], o_free(n + 1))
                        pe.wait_ge(s["og_done"], og_done(n))
                        ins = nc.tensor.matmul(k.ln_ps[:, 0, 0:T], cst[:, SEL, :], os_[:, n % 2, :], start=True, stop=True)
                        ins.then_inc(s["r_done"], 1)

                    for h, (a, g, j) in enumerate(heads):
                        if j == 0:
                            pe.wait_ge(s["px_free"], px_free(x))
                            settle(pe, k)
                            q0 = T - 1 if causal else 0
                            for jj in range(J4):
                                r = slice(32 * jj, 32 * jj + 32)
                                ins = nc.tensor.matmul(px[r, q0:T], qk[r, 1 + a, g, 256:288], qk[r, 0, g, q0:T], start=True, stop=True)
                            ins.then_inc(s["px_done"], 1)
                            x += 1
                        r = slice(32 * j, 32 * j + 32)
                        pe.wait_ge(s["pa_free"], pa_free(n - 1))
                        for t in range(2):
                            q0 = P * t if causal else 0
                            ins = nc.tensor.matmul(pa[:, n % 2, t, q0:T], qk[r, 1 + a, g, t * P:t * P + P], qk[r, 0, g, q0:T], start=True, stop=not causal)
                            if causal:
                                ins = nc.tensor.matmul(pa[:, n % 2, t, q0:q0 + P], k.ident[:], cst[:, MK, :], start=False, stop=True)
                        ins.then_inc(s["pa_done"], 1)
                        n += 1
                        if h:
                            values(h - 1)
                        if j == 2 and h > 4:
                            denominators(a * G + g - 1)
                    values(len(heads) - 1)
                    denominators(G * A - 1)
                    assert n == NT and x == NX
                    pe.wait_ge(s["og_done"], og_done(G * A))
                    for c in range(C):
                        for g in range(G):
                            ins = nc.tensor.matmul(k.ln_ps[:, c, 0:T], wo[:, g, c * P:c * P + P], og[:, g, :], start=(g == 0), stop=(g == G - 1))
                    ins.then_inc(s["y_done"], 1)

            @block.scalar
            def _(act):
                ln_scalar(act)
                with act.Fori(0, B) as i:
                    pa_free, pa_done = Turn(i, NT, 2), Turn(i, NT)
                    px_free, px_done = Turn(i, NX, 1), Turn(i, NX)
                    o_free, o_done = Turn(i, G * A, 1), Turn(i, G * A)
                    exp_done, og_done = Turn(i, NS), Turn(i, G * A + 1, 1)
                    n = 0
                    for g in range(G):
                        for m in range(NQ):
                            if not rope:
                                act.wait_ge(s["pa_done"], pa_done(n + 1))
                                if m == 0:
                                    ins = nc.scalar.copy(qk[:, 0, g, 0:T], pa[:, n % 2, 0, 0:T])
                                else:
                                    ins = nc.scalar.activation(qk[:, m, g, 0:T], pa[:, n % 2, 0, 0:T], ACT.Identity, bias=ind[:, m - 1:m])
                                ins.then_inc(s["pa_free"], 1)
                            n += 1
                    if not rope:
                        act.wait_ge(s["pa_done"], pa_done(n + 1))
                        ins = nc.scalar.copy(va[:, :, :, 0:DH], pa[:, n % 2, :, 0:D].rearrange("p t (h d) -> p t h d", d=DH))
                        ins.then_inc(s["pa_free"], 1)
                        act.wait_ge(s["pa_done"], pa_done(n + 2))
                        ins = nc.scalar.copy(vl[:, :, 0:DH], pa[:, (n + 1) % 2, 0, 0:D].rearrange("p (h d) -> p h d", d=DH))
                        ins.then_inc(s["pa_free"], 1)
                    n += 2 + NS
                    x = G * A + G
                    heads = [(a, g, j) for a in range(A) for g in range(G) for j in range(J4)]

                    def out_copy(m):
                        act.wait_ge(s["o_done"], o_done(m + 1))
                        act.wait_ge(s["og_done"], og_done(m - 1)) if m else None
                        nc.scalar.copy(os_[:, m % 2, :], po[:, 0:T]).then_inc(s["o_free"], 1)

                    for h, (a, g, j) in enumerate(heads):
                        if j == 0:
                            act.wait_ge(s["px_done"], px_done(x + 1))
                            q0 = T - 1 if causal else 0
                            nc.scalar.activation(pl[:, g % 2, q0:T], px[:, q0:T], ACT.Exp, scale=scale).then_inc(s["px_free"], 1)
                            x += 1
                        act.wait_ge(s["pa_done"], pa_done(n + 1))
                        act.wait_ge(s["px_free"], px_free(x))
                        if causal:
                            nc.scalar.activation(pe_p[:, h % 2, 0, :], pa[:, n % 2, 0, 0:T], ACT.Exp, scale=scale)
                            ins = nc.scalar.activation(pe_p[:, h % 2, 1, P:T], pa[:, n % 2, 1, P:T], ACT.Exp, scale=scale)
                        else:
                            ins = nc.scalar.activation(pe_p[:, h % 2], pa[:, n % 2, :, 0:T], ACT.Exp, scale=scale)
                        ins.then_inc(s["pa_free"], 1)
                        act.wait_ge(s["pa_free"], pa_free(n + 1))
                        act.sem_inc(s["exp_done"], 1)
                        n += 1
                        if j == 0 and h:
                            out_copy(a * G + g - 1)
                    out_copy(G * A - 1)

            @block.vector
            def _(dve):
                nc.vector.memset(mp[:], 0.0)
                nc.vector.memset(qk[:, :, :, T:TL], 0.0)
                nc.vector.memset(va[:, :, :, DH:32], 1.0)
                ini = nc.vector.memset(vl[:, :, DH:32], 1.0)
                link = Link(dve, k.dve_link)
                link(ini)
                ln_vector(dve)
                dve.wait_ge(k.ln_free, B + 1)
                dve.wait_ge(s["w_ready"], 1)
                if alpha is not None:
                    link(nc.vector.tensor_scalar(al[:, 1:2], al[:, 0:1], -1.0, 1.0, ALU.mult, ALU.add))
                dve.sem_inc(s["fold_out"], 1)
                if fold:
                    for m in range(3):
                        for c in range(C):
                            dve.wait_ge(s["fold_done"], m * C + c + 1)
                            for hh in range(2):
                                src = pa[:, hh, 0, :].rearrange("p (h w) -> p h w", w=64)
                                if m < 2:
                                    for r in range(2):
                                        ins = nc.vector.tensor_copy(wqk[:, m, r, c, hh * 256:hh * 256 + 256].rearrange("p (h w) -> p h w", w=32), src[:, :, r * 32:r * 32 + 32])
                                else:
                                    ins = nc.vector.tensor_copy(wv[:, c, hh * P:hh * P + P].rearrange("p (h w) -> p h w", w=DH), src[:, :, 0:DH])
                            ins.then_inc(s["fold_out"], 1)
                else:
                    dve.sem_inc(s["fold_out"], 6)
                dve.sem_inc(s["x_free"], 1)
                dve.sem_inc(s["pa_free"], 2)
                dve.sem_inc(s["px_free"], 1)
                dve.sem_inc(s["o_free"], 1)
                dve.sem_inc(s["og_done"], 1)
                per = (3 * G * NQ - G if rope else 0) + 2 * G * A - G * (A - 1) * 0
                with dve.Fori(0, B) as i:
                    pa_free, pa_done = Turn(i, NT, 2), Turn(i, NT)
                    px_free, px_done = Turn(i, NX, 1), Turn(i, NX)
                    r_done, og_done = Turn(i, G * A), Turn(i, G * A + 1, 1)
                    n, x, nl = 0, 0, 0
                    link.enter(i, DVE_LINKS(rope, A))
                    if rope:
                        for g in range(G):
                            for m in range(NQ):
                                dve.wait_ge(s["pa_done"], pa_done(n + 1))
                                nc.vector.tensor_tensor(t1[:], pa[:, n % 2, 0, 0:T], rp[:, 0, :], ALU.mult)
                                link(nc.vector.tensor_tensor(rc[:], pa[:, n % 2, 1, 0:T], rp[:, 1, :], ALU.mult))
                                if m == 0:
                                    ins = nc.vector.tensor_tensor(qk[:, 0, g, 0:T], t1[:], rc[:], ALU.add)
                                else:
                                    ins = nc.vector.scalar_tensor_tensor(out=qk[:, m, g, 0:T], in0=t1[:], scalar=ind[:, m - 1:m], in1=rc[:], op0=ALU.add, op1=ALU.add)
                                ins.then_inc(s["pa_free"], 1)
                                dve.wait_ge(s["pa_free"], pa_free(n + 1))
                                n += 1
                        dve.wait_ge(s["pa_done"], pa_done(n + 1))
                        nc.vector.tensor_copy(va[:, :, :, 0:DH], pa[:, n % 2, :, 0:D].rearrange("p t (h d) -> p t h d", d=DH)).then_inc(s["pa_free"], 1)
                        dve.wait_ge(s["pa_done"], pa_done(n + 2))
                        nc.vector.tensor_copy(vl[:, :, 0:DH], pa[:, (n + 1) % 2, 0, 0:D].rearrange("p (h d) -> p h d", d=DH)).then_inc(s["pa_free"], 1)
                        n += 2
                    else:
                        n = NU
                    for a in range(A):
                        for g in range(G):
                            dve.wait_ge(s["px_done"], px_done(x + 1))
                            nc.vector.tensor_reduce(ml[:, a, g:g + 1], px[:, 0:T], AX, ALU.max).then_inc(s["px_free"], 1)
                            x += 1
                            for j in range(J4):
                                dve.wait_ge(s["pa_done"], pa_done(n + 1))
                                col = 32 * j + DH + a
                                if causal:
                                    nc.vector.tensor_reduce(mp[:, 0, g, col:col + 1], pa[:, n % 2, 0, 0:P], AX, ALU.max)
                                    ins = nc.vector.tensor_reduce(mp[:, 1, g, col:col + 1], pa[:, n % 2, 1, 0:2 * P], AX, ALU.max)
                                else:
                                    ins = nc.vector.tensor_reduce(mp[:, :, g, col:col + 1], pa[:, n % 2, :, 0:T], AX, ALU.max)
                                ins.then_inc(s["pa_free"], 1)
                                n += 1
                    dve.sem_inc(s["x_free"], 1)
                    for g in range(G):
                        dve.wait_ge(s["px_done"], px_done(x + 1))
                        nc.vector.tensor_tensor(qk[:, 0, g, 0:T], qk[:, 0, g, 0:T], px[:, 0:T], ALU.add).then_inc(s["px_free"], 1)
                        x += 1
                    dve.wait_ge(s["px_free"], px_free(x))
                    dve.sem_inc(s["qk_set"], 1)
                    for a in range(A):
                        for g in range(G):
                            m = a * G + g
                            dve.wait_ge(s["r_done"], r_done(m + 1))
                            link(nc.vector.reciprocal(rc[:], k.ln_ps[:, 0, 0:T]))
                            if A == 1:
                                ins = nc.vector.tensor_tensor(og[:, g, :], os_[:, m % 2, :], rc[:], ALU.mult)
                            elif a == 0:
                                ins = nc.vector.scalar_tensor_tensor(out=og[:, g, :], in0=os_[:, m % 2, :], scalar=al[:, 0:1], in1=rc[:], op0=ALU.mult, op1=ALU.mult)
                            else:
                                link(nc.vector.scalar_tensor_tensor(out=t1[:], in0=os_[:, m % 2, :], scalar=al[:, 1:2], in1=rc[:], op0=ALU.mult, op1=ALU.mult))
                                ins = nc.vector.tensor_tensor(og[:, g, :], og[:, g, :], t1[:], ALU.add)
                            ins.then_inc(s["og_done"], 1)
                            dve.wait_ge(s["og_done"], og_done(m + 1))
                    dve.wait_ge(s["y_done"], i + 1)
                    hb = k.h[:, :, bass.ds(i, 1), :].rearrange("p c o t -> p c (o t)")
                    nc.vector.tensor_tensor(hb, hb, k.ln_ps[:, :, 0:T], ALU.add).then_inc(s["og_done"], 1)
                    dve.wait_ge(s["og_done"], og_done(G * A + 1))
                link.leave(B)
        clear(nc, k, s.values())


def DVE_LINKS(rope, A):
    return (G * 2 if rope else 0) + G * A + (G if A == 2 else 0)


def route_images(nc, k, s, r, E, w_r, top, p_l, p_t, gates, order):
    mx, ix, fx, hot, g, e = r["mx"], r["ix"], r["fx"], r["hot"], r["g"], r["e"]

    def pool_body(pool, i):
        if order is not None:
            pool.wait_ge(order, i + 2)
        pool.wait_ge(s["xb_free"], i + 1)
        nc.gpsimd.tensor_copy(k.xb[:, :, 0:T], k.x[:, :, bass.ds(i, 1), :].rearrange("p c o t -> p c (o t)")).then_inc(s["x_in"], 1)

    def tensor_body(pe, i):
        pe.wait_ge(s["x_in"], i + 1)
        pe.wait_ge(s["l_free"], i + 1)
        for t in range(3):
            for c in range(C):
                ins = nc.tensor.matmul(p_l[:, t * E:t * E + E], k.xb[:, c, t * P:t * P + P], w_r[:, c, :], start=(c == 0), stop=(c == C - 1))
        ins.then_inc(s["logits"], 1)
        pe.wait_ge(s["gated"], i + 1)
        pe.wait_ge(s["t_free"], i + 1)
        for t in range(3):
            ins = nc.tensor.transpose(p_t[0:E, t * P:t * P + P], g[:, t, :], k.ident[:])
        ins.then_inc(s["turned"], 1)

    def scalar_body(act, i):
        if top != "one":
            act.wait_ge(s["e_in"], i + 1)
            nc.scalar.activation(e[:], e[:], ACT.Exp).then_inc(s["e_out"], 1)
        act.wait_ge(s["turned"], i + 1)
        nc.scalar.copy(gates[0:E, bass.ds(i, 1), :].rearrange("e o t -> e (o t)"), p_t[0:E, 0:T]).then_inc(s["t_free"], 1)

    def vector_body(dve, link, i):
        dve.wait_ge(s["logits"], i + 1)
        lgs = r["lg"]
        if top == "one":
            link(nc.vector.tensor_tensor(lgs[:], p_l[:, 0:3 * E].rearrange("p (t e) -> p t e", t=3), r["rb"][:].unsqueeze(1).broadcast_to([P, 3, E]), ALU.add))
        else:
            link(nc.vector.tensor_copy(lgs[:], p_l[:, 0:3 * E].rearrange("p (t e) -> p t e", t=3)))
        dve.sem_inc(s["l_free"], 1)
        dve.sem_inc(s["xb_free"], 1)
        for t in range(3):
            settle(dve, k)
            link(nc.vector.max(mx[:, t, :], lgs[:, t, :]))
        for t in range(3):
            settle(dve, k)
            link(nc.vector.max_index(ix[:, t, :], mx[:, t, :], lgs[:, t, :]))
        if top == "softmax2":
            nc.vector.tensor_tensor(e[:], mx[:, :, 1:2], mx[:, :, 0:1], ALU.subtract).then_inc(s["e_in"], 1)
        if top == "sigmoid1":
            nc.vector.tensor_scalar_mul(e[:], mx[:, :, 0:1], -1.0).then_inc(s["e_in"], 1)
        link(nc.vector.tensor_copy(fx[:], ix[:, :, 0:2]))
        n = 2 if top == "softmax2" else 1
        io = r["iota"][:].unsqueeze(1).broadcast_to([P, 3, E])
        for j in range(n):
            link(nc.vector.tensor_tensor(hot[:, j], io, fx[:, :, j:j + 1].broadcast_to([P, 3, E]), ALU.is_equal))
        dve.wait_ge(s["t_free"], i + 1)
        if top == "one":
            nc.vector.tensor_copy(g[:], hot[:, 0]).then_inc(s["gated"], 1)
            return
        dve.wait_ge(s["e_out"], i + 1)
        link(nc.vector.tensor_scalar_add(mx[:, :, 0:1], e[:], 1.0))
        link(nc.vector.reciprocal(mx[:, :, 0:1], mx[:, :, 0:1]))
        if top == "sigmoid1":
            nc.vector.tensor_tensor(g[:], hot[:, 0], mx[:, :, 0:1].broadcast_to([P, 3, E]), ALU.mult).then_inc(s["gated"], 1)
            return
        link(nc.vector.tensor_tensor(mx[:, :, 1:2], e[:], mx[:, :, 0:1], ALU.mult))
        for j in range(2):
            link(nc.vector.tensor_tensor(hot[:, j], hot[:, j], mx[:, :, j:j + 1].broadcast_to([P, 3, E]), ALU.mult))
        nc.vector.tensor_tensor(g[:], hot[:, 0], hot[:, 1], ALU.add).then_inc(s["gated"], 1)

    links = {"softmax2": 15, "sigmoid1": 11, "one": 9}[top]
    return pool_body, tensor_body, scalar_body, vector_body, links


ROUTE_SIGS = "x_in xb_free l_free logits gated t_free turned e_in e_out".split()


def route_tiles(sb, E):
    r = {n: sb(n, sh) for n, sh in (("lg", [P, 3, E]), ("mx", [P, 3, 8]), ("fx", [P, 3, 2]), ("hot", [P, 2, 3, E]),
                                    ("g", [P, 3, E]), ("e", [P, 3, 1]), ("iota", [P, E]), ("rb", [P, E]))}
    r["ix"] = sb("ix", [P, 3, 8], U32)
    return r


def section_moe(nc, k, tag, E, top, w_router, w_up, w_down, iota, scale=None, shared=False):
    HID = 512
    J = HID // P
    NE = E + (1 if shared else 0)
    rms = top == "softmax2"
    with ExitStack() as ctx:
        sb = lambda name, shape, dt=F32: ctx.enter_context(nc.sbuf_tensor(tag + "_" + name, shape, dt))
        ps = lambda name, shape: ctx.enter_context(nc.psum_tensor(tag + "_" + name, shape, F32))
        r = route_tiles(sb, E)
        w_r = sb("wr", [P, C, E])
        gates = sb("gates", [NE, B, T])
        up = sb("up", [P, 2, C, 2 * HID])
        down = sb("down", [P, 2, J, D])
        gb = sb("gb", [P, 2, B, T])
        xs = None if rms else sb("xs", [P, 2, 2, C, T])
        D0 = 0 if rms else 4
        act_g = sb("actg", [P, 2, T])
        hid = sb("hid", [P, 2, 2, T])
        tmp = sb("tmp", [P, 2, C, T])
        sc = sb("sc", [P, C])
        p_h = ps("ph", [P, 2, 2, BANK])
        p_d0 = ps("pd", [P, C, BANK])
        p_d = [k.ln_ps, p_d0]
        p_l, p_t = p_h[:, 0, 0, :], p_h[:, 0, 1, :]
        p_m = p_h[:, 1, 0, :]
        g_dram = nc.dram_tensor(tag + "_gates_dram", [NE, B * T], F32).ap()
        names = ROUTE_SIGS + "r_in g_set g_out w_in0 w_in1 xs_in scaled up_done act_done h_done d_done d_free rms_sq rms_ms rms_std rms_x".split()
        s = {n: signal(nc, ctx, tag + "_" + n) for n in names}
        ln_tensor, ln_scalar, ln_vector = layer_norm(nc, k, None)
        order = s["rms_x"] if rms else None
        pool_body, tensor_body, scalar_body, vector_body, links = route_images(
            nc, k, s, r, E, w_r, top, p_l, p_t, gates, order)
        n_r = 3 if rms else 2
        with nc.Block() as block:
            @block.sync
            def _(sp):
                sp.dma_start(w_r[:], w_router).then_inc(s["r_in"], 16)
                sp.dma_start(r["iota"][:], iota[0:E].partition_broadcast(P)).then_inc(s["r_in"], 16)
                if rms:
                    sp.dma_start(sc[:], scale).then_inc(s["r_in"], 16)
                def load(e, u, win):
                    sp.dma_start(up[:, u], w_up[e] if isinstance(e, int) else w_up[bass.ds(e, 1)].rearrange("o p c f -> p (o c) f")).then_inc(win, 16)
                    sp.dma_start(down[:, u], w_down[e] if isinstance(e, int) else w_down[bass.ds(e, 1)].rearrange("o p c f -> p (o c) f")).then_inc(win, 16)
                sp.wait_ge(s["t_free"], B + 1)
                sp.dma_start(g_dram, gates[:].rearrange("e b t -> e (b t)")).then_inc(s["g_out"], 16)
                sp.wait_ge(s["g_out"], 16)
                def load_e(e, u, win):
                    load(e, u, win)
                    row = g_dram[e] if isinstance(e, int) else g_dram[bass.ds(e, 1)].rearrange("o n -> (o n)")
                    sp.dma_start(gb[:, u].rearrange("p b t -> p (b t)"), row.partition_broadcast(P)).then_inc(win, 16)
                for u in range(2):
                    load_e(u, u, s["w_in%d" % u])
                NP = (NE - 2) // 2
                with sp.Fori(0, NP) as n:
                    for u in range(2):
                        sp.wait_ge(s["d_free"], (2 * n + u + 1) * B + 2)
                        load_e(2 * n + 2 + u, u, s["w_in%d" % u])
                if NE % 2:
                    sp.wait_ge(s["d_free"], (NE - 2) * B + 2)
                    load_e(NE - 1, 0, s["w_in0"])

            @block.gpsimd
            def _(pool):
                pool.wait_ge(k.ln_free, B + 1)
                with pool.Fori(0, B) as i:
                    pool_body(pool, i)
                if rms:
                    return
                pool.sem_inc(s["d_done"], D0)
                pool.wait_ge(s["t_free"], B + 1)

                def feed(n, q, v, u):
                    pool.wait_ge(s["d_done"], 2 * n + 1)
                    for o in range(2):
                        xo = k.x[:, :, bass.ds(q * 2 + o, 1), :].rearrange("p c o t -> p c (o t)")
                        go = gb[:, u, bass.ds(q * 2 + o, 1), :].broadcast_to([P, C, T])
                        ins = nc.gpsimd.tensor_tensor(xs[:, v, o], xo, go, ALU.mult)
                    ins.then_inc(s["xs_in"], 1)

                with pool.Fori(0, NE // 2) as m:
                    for u in range(2):
                        pool.wait_ge(s["w_in%d" % u], (m + 1) * 48)
                        settle(pool, k)
                        with pool.Fori(0, B // 4) as q:
                            for v in range(2):
                                feed((2 * m + u) * (B // 2) + 2 * q + v, 2 * q + v, v, u)
                if NE % 2:
                    pool.wait_ge(s["w_in0"], (NE // 2 + 1) * 48)
                    with pool.Fori(0, B // 4) as q:
                        for v in range(2):
                            feed((NE - 1) * (B // 2) + 2 * q + v, 2 * q + v, v, 0)

            @block.tensor
            def _(pe):
                ln_tensor(pe)
                pe.wait_ge(s["r_in"], 16 * n_r)
                with pe.Fori(0, B) as i:
                    if rms:
                        pe.wait_ge(s["rms_sq"], i + 1)
                        for c in range(C):
                            ins = nc.tensor.matmul(p_m[:, 0:T], k.mean[:], k.ln_sq[:, c, :], start=(c == 0), stop=(c == C - 1))
                        ins.then_inc(s["rms_ms"], 1)
                    tensor_body(pe, i)
                pe.wait_ge(s["t_free"], B + 1)
                pe.wait_ge(s["l_free"], B + 1)

                def pair(n, q, v, u):
                    if not rms:
                        pe.wait_ge(s["xs_in"], n + 1)
                    for j in range(J):
                        for o in range(2):
                            pe.wait_ge(s["h_done"], n * (2 * J) + 2 * j + o + 1)
                            for m in range(2):
                                for c in range(C):
                                    ins = nc.tensor.matmul(p_h[:, o, m, 0:T], up[:, u, c, m * HID + j * P:m * HID + j * P + P],
                                                           k.x[:, c, bass.ds(q * 2 + o, 1), :] if rms else xs[:, v, o, c, :], start=(c == 0), stop=(c == C - 1))
                            ins.then_inc(s["up_done"], 1)
                        if j:
                            down_half(n, j - 1, u)
                    down_half(n, J - 1, u)

                def down_half(n, j, u):
                    for o in range(2):
                        pe.wait_ge(s["h_done"], n * (2 * J) + 2 * j + o + 3)
                        if j == 0:
                            pe.wait_ge(s["d_free"], 2 * n + o + 1)
                        for c in range(C):
                            ins = nc.tensor.matmul(p_d[o][:, c, 0:T], down[:, u, j, c * P:c * P + P], hid[:, o, j % 2, :],
                                                   start=(j == 0), stop=(j == J - 1))
                        if j == J - 1:
                            ins.then_inc(s["d_done"], 1)

                with pe.Fori(0, NE // 2) as m:
                    for u in range(2):
                        pe.wait_ge(s["w_in%d" % u], (m + 1) * 48)
                        settle(pe, k)
                        with pe.Fori(0, B // 4) as q:
                            for v in range(2):
                                pair((2 * m + u) * (B // 2) + 2 * q + v, 2 * q + v, v, u)
                if NE % 2:
                    pe.wait_ge(s["w_in0"], (NE // 2 + 1) * 48)
                    with pe.Fori(0, B // 4) as q:
                        for v in range(2):
                            pair((NE - 1) * (B // 2) + 2 * q + v, 2 * q + v, v, 0)

            @block.scalar
            def _(act):
                ln_scalar(act)
                link = Link(act, k.act_link)
                act.sem_inc(s["t_free"], 1)
                act.wait_ge(k.ln_free, B + 1)
                with act.Fori(0, B) as i:
                    if rms:
                        link.enter(i, 1)
                        nc.scalar.activation(k.ln_sq[:], k.x[:, :, bass.ds(i, 1), :].rearrange("p c o t -> p c (o t)"), ACT.Square).then_inc(s["rms_sq"], 1)
                        act.wait_ge(s["rms_ms"], i + 1)
                        act.wait_ge(s["rms_x"], i + 1)
                        link(nc.scalar.activation(k.ln_rstd[:], p_m[:, 0:T], ACT.Ln, bias=k.eps[:, 1:2]))
                        nc.scalar.activation(k.ln_rstd[:], k.ln_rstd[:], ACT.Exp, scale=-0.5).then_inc(s["rms_std"], 1)
                    scalar_body(act, i)
                if rms:
                    link.leave(B)

                with act.Fori(0, NE * (B // 2)) as n:
                    for j in range(J):
                        for o in range(2):
                            act.wait_ge(s["up_done"], n * 2 * J + 2 * j + o + 1)
                            nc.scalar.activation(act_g[:, o, :], p_h[:, o, 1, 0:T], ACT.Silu).then_inc(s["act_done"], 1)

            @block.vector
            def _(dve):
                ln_vector(dve)
                link = Link(dve, k.dve_link)
                dve.sem_inc(s["l_free"], 1)
                dve.sem_inc(s["xb_free"], 1)
                dve.sem_inc(s["rms_x"], 1)
                dve.wait_ge(k.ln_free, B + 1)
                link(nc.vector.memset(gates[:], 1.0))
                dve.wait_ge(s["r_in"], 16 * n_r)
                with dve.Fori(0, B) as i:
                    link.enter(i, links + (3 if rms else 0))
                    if rms:
                        hb = k.h[:, :, bass.ds(i, 1), :].rearrange("p c o t -> p c (o t)")
                        xo = k.x[:, :, bass.ds(i, 1), :].rearrange("p c o t -> p c (o t)")
                        link(nc.vector.tensor_tensor(hb, hb, xo, ALU.add))
                        dve.wait_ge(s["rms_std"], i + 1)
                        link(nc.vector.tensor_tensor(xo, xo, k.ln_rstd[:].unsqueeze(1).broadcast_to([P, C, T]), ALU.mult))
                        for c in range(C):
                            ins = nc.vector.tensor_scalar_mul(k.x[:, c, bass.ds(i, 1), :], k.x[:, c, bass.ds(i, 1), :], sc[:, c:c + 1])
                        link(ins)
                        dve.sem_inc(s["rms_x"], 1)
                    vector_body(dve, link, i)
                link.leave(B)
                for _o in range(2):
                    dve.sem_inc(s["d_free"], 1)
                    dve.sem_inc(s["h_done"], 1)

                def pair(n, q, u):
                    for j in range(J):
                        for o in range(2):
                            dve.wait_ge(s["act_done"], n * 2 * J + 2 * j + o + 1)
                            nc.vector.tensor_tensor(hid[:, o, j % 2, :], p_h[:, o, 0, 0:T], act_g[:, o, :], ALU.mult).then_inc(s["h_done"], 1)
                    for o in range(2):
                        dve.wait_ge(s["d_done"], 2 * n + o + 1 + D0)
                        hb = k.h[:, :, bass.ds(q * 2 + o, 1), :].rearrange("p c o t -> p c (o t)")
                        if rms:
                            go = gb[:, u, bass.ds(q * 2 + o, 1), :].broadcast_to([P, C, T])
                            nc.vector.tensor_tensor(tmp[:, o], p_d[o][:, :, 0:T], go, ALU.mult).then_inc(s["scaled"], 1)
                            dve.wait_ge(s["scaled"], 2 * n + o + 1)
                            nc.vector.tensor_tensor(hb, hb, tmp[:, o], ALU.add).then_inc(s["d_free"], 1)
                        else:
                            nc.vector.tensor_tensor(hb, hb, p_d[o][:, :, 0:T], ALU.add).then_inc(s["d_free"], 1)

                with dve.Fori(0, NE // 2) as m:
                    for u in range(2):
                        dve.wait_ge(s["w_in%d" % u], (m + 1) * 48)
                        settle(dve, k)
                        with dve.Fori(0, B // 2) as q:
                            pair((2 * m + u) * (B // 2) + q, q, u)
                if NE % 2:
                    dve.wait_ge(s["w_in0"], (NE // 2 + 1) * 48)
                    with dve.Fori(0, B // 2) as q:
                        pair((NE - 1) * (B // 2) + q, q, 0)
        clear(nc, k, s.values())


DI, NS_, RK, KC = 512, 32, 16, 4
DJ = DI // P
NQ_ = 8
QN = NS_ // NQ_
TU = T + KC - 1


def section_mamba(nc, k, con, dirs, bfuse):
    with ExitStack() as ctx:
        sb = lambda name, shape, dt=F32: ctx.enter_context(nc.sbuf_tensor("ssm_" + name, shape, dt))
        ps = lambda name, shape: ctx.enter_context(nc.psum_tensor("ssm_" + name, shape, F32))
        w_in, w_x = sb("win", [P, C, 2 * DI]), sb("wx", [P, DJ, 2 * NS_ + RK])
        w_dt = sb("wdt", [2 * NS_ + RK, DI])
        w_out, w_fu = sb("wout", [P, DJ, D]), sb("wfu", [P, C, D])
        cols = sb("cols", [P, DJ, KC + 3])
        a_n = sb("an", [P, DJ, NS_])
        lnc = sb("lnc", [P, 3, C])
        eye3 = sb("eye3", [3 * NS_, NS_])
        sel = sb("sel", [3 * NS_, NS_, P], BF16)
        u_in = sb("uin", [P, DJ, TU])
        uc2, zs2, dt2, dtu2 = (sb(n, [P, 2, DJ, T]) for n in ("uc", "zs", "dt", "dtu"))
        bc_r = sb("bcr", [2 * NS_, T])
        part = sb("part", [2 * NS_, 3, T], BF16)
        bst2, cst2 = sb("bst", [3 * NS_, 2, T], BF16), sb("cst", [3 * NS_, 2, T], BF16)
        rank = sb("rank", [2 * NS_ + RK, T])
        cb = sb("cb", [P, NS_, T])
        da = sb("da", [P, 2, NQ_, T])
        hs = sb("hs", [P, 2, NQ_, T])
        hc = sb("hc", [P, 2, NQ_, T])
        half = sb("half", [P, 2, NQ_ // 2, T])
        e1, e2 = sb("e1", [P, DJ, T]), sb("e2", [P, DJ, T])
        pb = ps("pb", [P, 4, BANK])
        py = ps("py", [P, 2, BANK])
        pm = k.ln_ps
        names = ("w_in sel_set rates x_in x_free proj_done proj_free conv_done uc_done xd_done xd_out parts stacked dt_done "
                 "dt_free dt_exp dt_set c_done c_free b_done b_free da_done h_done hc_done half_done y_free ys_done o_done o_out "
                 "t_done cent sqd var std normed f_done f_out head_link tail_link main_link act_head act_tail").split()
        s = {n: signal(nc, ctx, "ssm_" + n) for n in names}
        ln_tensor, ln_scalar, ln_vector = layer_norm(nc, k, None)
        NCH = DJ * QN

        def images(eng, body):
            body(0, 0, False, True)
            with eng.Fori(0, (B - 2) // 2) as m:
                body(2 * m + 1, 1, True, True)
                body(2 * m + 2, 0, True, True)
            body(B - 1, 1, True, False)

        def per_image(eng, sem, i, per):
            n = [0]

            def link(ins):
                n[0] += 1
                assert n[0] <= per
                ins.then_inc(sem, 1)
                eng.wait_ge(sem, i * per + n[0])
            return link

        for d, w in enumerate(dirs):
            n_w = 9 + (d == 0)
            with nc.Block() as block:
                @block.sync
                def _(sp):
                    for dst, src in ((w_in[:], w["win"]), (w_x[:], w["wx"]), (w_dt[2 * NS_:], w["wdt"]), (w_out[:], w["wout"]),
                                     (w_fu[:], w["wfu"]), (cols[:], w["cols"]), (a_n[:], w["alog"]), (lnc[:, 0:2], w["ln"]),
                                     (lnc[:, 2], bfuse)):
                        sp.dma_start(dst, src).then_inc(s["w_in"], 16)
                    if d == 0:
                        sp.dma_start(eye3[:], con["sel"]).then_inc(s["w_in"], 16)

                @block.gpsimd
                def _(pool):
                    if d == 0:
                        pool.wait_ge(k.ln_free, B + 1)
                    pool.sem_inc(s["hc_done"], 2)

                    def take(i):
                        dst = k.xb[:, :, 0:T] if d == 0 else k.xb[:, :, T - 1::-1]
                        nc.gpsimd.tensor_copy(dst, k.x[:, :, bass.ds(i, 1), :].rearrange("p c o t -> p c (o t)")).then_inc(s["x_in"], 1)

                    def body(i, v, before, after):
                        h_done, halved, c_free = Turn(i, NCH, 2), Turn(i, NCH, 2), Turn(i, NS_, 2)
                        for n in range(NCH):
                            j, q = n // QN, n % QN
                            if n == 2 and after:
                                pool.wait_ge(s["x_free"], i + 1)
                                settle(pool, k)
                                take(i + 1)
                            if j == 0:
                                pool.wait_ge(s["c_free"], c_free(NQ_ * (q + 1)))
                            pool.wait_ge(s["h_done"], h_done(n + 1))
                            pool.wait_ge(s["half_done"], halved(n - 1))
                            nc.gpsimd.tensor_tensor(hc[:, n % 2], hs[:, n % 2], cb[:, q * NQ_:(q + 1) * NQ_, :], ALU.mult).then_inc(s["hc_done"], 1)

                    take(0)
                    images(pool, body)

                @block.tensor
                def _(pe):
                    if d == 0:
                        ln_tensor(pe)
                        pe.wait_ge(s["sel_set"], 1)
                    pe.wait_ge(s["w_in"], 16 * n_w)

                    def project(i, lo_, hi_):
                        pf = Turn(i, 8, 2)
                        for n in range(lo_, hi_):
                            pe.wait_ge(s["proj_free"], pf(n - 1))
                            for c in range(C):
                                ins = nc.tensor.matmul(pm[:, n % 2, 0:T], w_in[:, c, n * P:n * P + P], k.xb[:, c, 0:T], start=(c == 0), stop=(c == C - 1))
                            ins.then_inc(s["proj_done"], 1)

                    def b_c_rank(i, v):
                        pe.wait_ge(s["proj_free"], Turn(i, 8, 2)(8))
                        pe.wait_ge(s["uc_done"], i + 1)
                        for j in range(DJ):
                            ins = nc.tensor.matmul(pm[0:2 * NS_ + RK, 0, 0:T], w_x[:, j, :], uc2[:, v, j, :], start=(j == 0), stop=(j == DJ - 1))
                        ins.then_inc(s["xd_done"], 1)

                    def time_step(i):
                        pe.wait_ge(s["xd_out"], i + 1)
                        pe.wait_ge(s["parts"], 3 * i + 2)
                        r = slice(2 * NS_, 2 * NS_ + RK)
                        df = Turn(i, DJ, 2)
                        for j in range(DJ):
                            pe.wait_ge(s["dt_free"], df(j - 1))
                            nc.tensor.matmul(pm[:, j % 2, 0:T], w_dt[r, j * P:j * P + P], rank[r, :], start=True, stop=True).then_inc(s["dt_done"], 1)

                    def spread_c(i, v, q):
                        cf = Turn(i, NS_, 2)
                        if q == 0:
                            pe.wait_ge(s["dt_free"], Turn(i, DJ, 2)(DJ))
                        for n in range(NQ_ * q, NQ_ * q + NQ_):
                            pe.wait_ge(s["c_free"], cf(n - 1))
                            nc.tensor.matmul(pm[:, n % 2, 0:T], sel[:, n, :], cst2[:, v, :], start=True, stop=True).then_inc(s["c_done"], 1)

                    def spread_b(i, v, n):
                        bf_ = Turn(i, 4 * NCH, 2)
                        for m in range(4):
                            pe.wait_ge(s["b_free"], bf_(4 * n + m - 1))
                            for o in range(2):
                                st = (n % QN) * NQ_ + 2 * m + o
                                ins = nc.tensor.matmul(pb[:, 2 * (m % 2) + o, 0:T], sel[:, st, :], bst2[:, v, :], start=True, stop=True)
                            ins.then_inc(s["b_done"], 1)

                    def total(i, n):
                        j, q = n // QN, n % QN
                        pe.wait_ge(s["half_done"], Turn(i, NCH, 2)(n + 1))
                        if q == 0:
                            pe.wait_ge(s["ys_done"], Turn(i, DJ, 2)(j - 1))
                        for m in range(NQ_ // 2):
                            ins = nc.tensor.matmul(py[:, j % 2, 0:T], k.ident[:], half[:, n % 2, m, :], start=(q == 0 and m == 0), stop=(q == QN - 1 and m == NQ_ // 2 - 1))
                        ins.then_inc(s["y_free"], 1)

                    def tail(i, v, step):
                        if step == 0:
                            pe.wait_ge(s["ys_done"], Turn(i, DJ, 2)(DJ))
                            for c in range(C):
                                for j in range(DJ):
                                    ins = nc.tensor.matmul(pm[:, c, 0:T], w_out[:, j, c * P:c * P + P], zs2[:, v, j, :], start=(j == 0), stop=(j == DJ - 1))
                            ins.then_inc(s["o_done"], 1)
                        if step == 1:
                            pe.wait_ge(s["o_out"], i + 1)
                            for c in range(C):
                                ins = nc.tensor.matmul(pm[:, 0, 0:T], k.mean[:], k.ln_sq[:, c, :], start=(c == 0), stop=(c == C - 1))
                            ins.then_inc(s["t_done"], 1)
                        if step == 2:
                            pe.wait_ge(s["sqd"], i + 1)
                            for c in range(C):
                                ins = nc.tensor.matmul(pm[:, 1, 0:T], k.mean[:], k.ln_sq[:, c, :], start=(c == 0), stop=(c == C - 1))
                            ins.then_inc(s["var"], 1)
                        if step == 3:
                            pe.wait_ge(s["normed"], i + 1)
                            for c in range(C):
                                for cc in range(C):
                                    ins = nc.tensor.matmul(pm[:, c, 0:T], w_fu[:, cc, c * P:c * P + P], k.ln_cen[:, cc, :], start=(cc == 0), stop=(cc == C - 1))
                            ins.then_inc(s["f_done"], 1)

                    def body(i, v, before, after):
                        pe.wait_ge(s["stacked"], i + 1)
                        for n in range(NCH):
                            spread_b(i, v, n)
                            if n < QN:
                                spread_c(i, v, n)
                            if before and n in (4, 5, 6, 8):
                                if n == 4:
                                    pe.wait_ge(s["c_free"], Turn(i, NS_, 2)(NS_))
                                tail(i - 1, 1 - v, {4: 0, 5: 1, 6: 2, 8: 3}[n])
                            if after:
                                if n == 9:
                                    if before:
                                        pe.wait_ge(s["f_out"], i)
                                    else:
                                        pe.wait_ge(s["c_free"], Turn(i, NS_, 2)(NS_))
                                    pe.wait_ge(s["x_in"], i + 2)
                                    project(i + 1, 0, 4)
                                if n == 11:
                                    project(i + 1, 4, 8)
                                if n == 12:
                                    b_c_rank(i + 1, 1 - v)
                                if n == 13:
                                    time_step(i + 1)
                            if n >= 2:
                                total(i, n - 2)
                        total(i, NCH - 2)
                        total(i, NCH - 1)

                    pe.wait_ge(s["x_in"], 1)
                    project(0, 0, 8)
                    b_c_rank(0, 0)
                    time_step(0)
                    images(pe, body)
                    pe.wait_ge(s["c_free"], Turn(B - 1, NS_, 2)(NS_))
                    for step in range(4):
                        tail(B - 1, 1, step)

                @block.scalar
                def _(act):
                    if d == 0:
                        ln_scalar(act)
                    link = Link(act, k.act_link)
                    act.wait_ge(s["w_in"], 16 * n_w)
                    act.wait_ge(s["rates"], 1)
                    link(nc.scalar.activation(a_n[:], a_n[:], ACT.Exp))
                    link(nc.scalar.mul(a_n[:], a_n[:], -1.0))
                    act.sem_inc(s["proj_free"], 2)
                    act.sem_inc(s["c_free"], 2)

                    def take_u(i):
                        for n in range(DJ):
                            act.wait_ge(s["proj_done"], Turn(i, 8)(n + 1))
                            nc.scalar.copy(u_in[:, n, KC - 1:TU], pm[:, n % 2, 0:T]).then_inc(s["proj_free"], 1)

                    def take_z(i, v):
                        for n in range(DJ):
                            act.wait_ge(s["proj_done"], Turn(i, 8)(DJ + n + 1))
                            nc.scalar.activation(zs2[:, v, n, :], pm[:, n % 2, 0:T], ACT.Silu).then_inc(s["proj_free"], 1)
                        act.wait_ge(s["conv_done"], i + 1)
                        nc.scalar.activation(uc2[:, v], e1[:], ACT.Silu).then_inc(s["uc_done"], 1)
                        act.preload_act_table_set("natural_log_exp_and_others")

                    def stack(i, v):
                        act.wait_ge(s["xd_done"], i + 1)
                        r = slice(2 * NS_, 2 * NS_ + RK)
                        nc.scalar.copy(rank[r, :], pm[r, 0, 0:T]).then_inc(s["xd_out"], 1)
                        act.wait_ge(s["parts"], 3 * i + 3)
                        for m in range(3):
                            nc.scalar.copy(bst2[NS_ * m:NS_ * m + NS_, v, :], part[0:NS_, m, :])
                            ins = nc.scalar.copy(cst2[NS_ * m:NS_ * m + NS_, v, :], part[NS_:2 * NS_, m, :])
                        ins.then_inc(s["stacked"], 1)

                    def soften(i, v):
                        hlink = per_image(act, s["act_head"], i, 2)
                        act.wait_ge(s["dt_free"], Turn(i, DJ, 2)(DJ))
                        hlink(nc.scalar.activation(e1[:], dt2[:, v], ACT.Abs))
                        hlink(nc.scalar.activation(e1[:], e1[:], ACT.Exp, scale=-1.0))
                        nc.scalar.activation(e2[:], e1[:], ACT.Ln, bias=k.ones[:, 0:1]).then_inc(s["dt_exp"], 1)

                    def tail(i, step):
                        if step == 0:
                            act.wait_ge(s["o_done"], i + 1)
                            nc.scalar.copy(k.ln_sq[:], pm[:, :, 0:T]).then_inc(s["o_out"], 1)
                        if step == 1:
                            act.wait_ge(s["cent"], i + 1)
                            nc.scalar.activation(k.ln_sq[:], k.ln_cen[:], ACT.Square).then_inc(s["sqd"], 1)
                        if step == 2:
                            act.wait_ge(s["var"], i + 1)
                            per_image(act, s["act_tail"], i, 1)(nc.scalar.activation(k.ln_rstd[:], pm[:, 1, 0:T], ACT.Ln, bias=k.eps[:, 0:1]))
                            nc.scalar.activation(k.ln_rstd[:], k.ln_rstd[:], ACT.Exp, scale=-0.5).then_inc(s["std"], 1)

                    def body(i, v, before, after):
                        act.wait_ge(s["dt_set"], i + 1)
                        for n in range(NCH):
                            j, q = n // QN, n % QN
                            act.wait_ge(s["h_done"], Turn(i, NCH, 2)(n - 1))
                            for m in range(NQ_):
                                st = q * NQ_ + m
                                ins = nc.scalar.activation(da[:, n % 2, m, 1:T], dt2[:, v, j, 1:T], ACT.Exp, scale=a_n[:, j, st:st + 1])
                            ins.then_inc(s["da_done"], 1)
                            if n < QN:
                                for m in range(NQ_ * n, NQ_ * n + NQ_):
                                    act.wait_ge(s["c_done"], Turn(i, NS_)(m + 1))
                                    nc.scalar.copy(cb[:, m, :], pm[:, m % 2, 0:T]).then_inc(s["c_free"], 1)
                            if before and n in (4, 6, 7):
                                tail(i - 1, {4: 0, 6: 1, 7: 2}[n])
                            if after:
                                if n == 9:
                                    take_u(i + 1)
                                if n == 11:
                                    take_z(i + 1, 1 - v)
                                if n == 12:
                                    stack(i + 1, 1 - v)
                                if n == 13:
                                    soften(i + 1, 1 - v)

                    take_u(0)
                    take_z(0, 0)
                    stack(0, 0)
                    soften(0, 0)
                    images(act, body)
                    for step in range(3):
                        tail(B - 1, step)

                @block.vector
                def _(dve):
                    if d == 0:
                        ln_vector(dve)
                        dve.wait_ge(k.ln_free, B + 1)
                    link = Link(dve, k.dve_link)
                    link(nc.vector.memset(u_in[:, :, 0:KC - 1], 0.0))
                    link(nc.vector.memset(da[:, :, :, 0:1], 0.0))
                    dve.wait_ge(s["w_in"], 16 * n_w)
                    if d == 0:
                        nc.vector.tensor_copy(sel[:], eye3[:].unsqueeze(2).broadcast_to([3 * NS_, NS_, P])).then_inc(s["sel_set"], 1)
                    nc.vector.tensor_scalar_min(a_n[:], a_n[:], 83.0).then_inc(s["rates"], 1)
                    dve.sem_inc(s["b_free"], 2)
                    dve.sem_inc(s["y_free"], 2)
                    dve.sem_inc(s["h_done"], 2)
                    dve.sem_inc(s["half_done"], 2)
                    dve.sem_inc(s["ys_done"], 2)
                    dve.sem_inc(s["dt_free"], 2)

                    def conv(i, hlink):
                        dve.wait_ge(s["proj_free"], Turn(i, 8, 2)(DJ))
                        for j in range(DJ):
                            ins = nc.vector.tensor_scalar(e1[:, j, :], u_in[:, j, 0:T], cols[:, j, 0:1], cols[:, j, KC:KC + 1], ALU.mult, ALU.add)
                        hlink(ins)
                        for m in range(1, KC):
                            for j in range(DJ):
                                ins = nc.vector.scalar_tensor_tensor(out=e1[:, j, :], in0=u_in[:, j, m:m + T], scalar=cols[:, j, m:m + 1], in1=e1[:, j, :], op0=ALU.mult, op1=ALU.add)
                            if m < KC - 1:
                                hlink(ins)
                        ins.then_inc(s["conv_done"], 1)

                    def split(i, hlink):
                        dve.wait_ge(s["xd_done"], i + 1)
                        r = slice(0, 2 * NS_)
                        hlink(nc.vector.tensor_copy(part[:, 0, :], pm[r, 0, 0:T]))
                        dve.sem_inc(s["x_free"], 1)
                        nc.vector.tensor_tensor(bc_r[:], pm[r, 0, 0:T], part[:, 0, :], ALU.subtract).then_inc(s["parts"], 1)
                        dve.wait_ge(s["parts"], 3 * i + 1)
                        nc.vector.tensor_copy(part[:, 1, :], bc_r[:]).then_inc(s["parts"], 1)
                        dve.wait_ge(s["parts"], 3 * i + 2)
                        hlink(nc.vector.tensor_tensor(bc_r[:], bc_r[:], part[:, 1, :], ALU.subtract))
                        nc.vector.tensor_copy(part[:, 2, :], bc_r[:]).then_inc(s["parts"], 1)

                    def take_dt(i, v):
                        for j in range(DJ):
                            dve.wait_ge(s["dt_done"], Turn(i, DJ)(j + 1))
                            nc.vector.tensor_scalar(dt2[:, v, j, :], pm[:, j % 2, 0:T], cols[:, j, KC + 1:KC + 2], None, ALU.add).then_inc(s["dt_free"], 1)

                    def soften(i, v, hlink):
                        dve.wait_ge(s["dt_exp"], i + 1)
                        hlink(nc.vector.tensor_scalar(dtu2[:, v], e1[:], -0.5, 1.0, ALU.mult, ALU.add))
                        hlink(nc.vector.tensor_tensor(e1[:], e1[:], dtu2[:, v], ALU.mult))
                        hlink(nc.vector.tensor_tensor(e1[:], e1[:], e2[:], ALU.max))
                        hlink(nc.vector.scalar_tensor_tensor(out=dt2[:, v], in0=dt2[:, v], scalar=0.0, in1=e1[:], op0=ALU.max, op1=ALU.add))
                        hlink(nc.vector.tensor_tensor(dtu2[:, v], dt2[:, v], uc2[:, v], ALU.mult))
                        dve.sem_inc(s["dt_set"], 1)

                    def halve(i, n):
                        dve.wait_ge(s["hc_done"], Turn(i, NCH, 2)(n + 1))
                        dve.wait_ge(s["y_free"], Turn(i, NCH, 2)(n - 1))
                        nc.vector.tensor_tensor(half[:, n % 2], hc[:, n % 2, 0:NQ_ // 2, :], hc[:, n % 2, NQ_ // 2:, :], ALU.add).then_inc(s["half_done"], 1)

                    def out_chunk(i, v, j):
                        dve.wait_ge(s["y_free"], Turn(i, NCH, 2)((j + 1) * QN))
                        nc.vector.scalar_tensor_tensor(out=uc2[:, v, j, :], in0=uc2[:, v, j, :], scalar=cols[:, j, KC + 2:KC + 3], in1=py[:, j % 2, 0:T], op0=ALU.mult, op1=ALU.add).then_inc(s["main_link"], 1)
                        dve.wait_ge(s["main_link"], Turn(i, DJ)(j + 1))
                        nc.vector.tensor_tensor(zs2[:, v, j, :], zs2[:, v, j, :], uc2[:, v, j, :], ALU.mult).then_inc(s["ys_done"], 1)

                    def tail(i, step):
                        if step == 0:
                            dve.wait_ge(s["t_done"], i + 1)
                            nc.vector.tensor_tensor(k.ln_cen[:], k.ln_sq[:], pm[:, 0, 0:T].unsqueeze(1).broadcast_to([P, C, T]), ALU.subtract).then_inc(s["cent"], 1)
                        if step == 1:
                            dve.wait_ge(s["std"], i + 1)
                            per_image(dve, s["tail_link"], i, 1)(nc.vector.tensor_tensor(k.ln_cen[:], k.ln_cen[:], k.ln_rstd[:].unsqueeze(1).broadcast_to([P, C, T]), ALU.mult))
                            for c in range(C):
                                ins = nc.vector.tensor_scalar(k.ln_cen[:, c, :], k.ln_cen[:, c, :], lnc[:, 0, c:c + 1], lnc[:, 1, c:c + 1], ALU.mult, ALU.add)
                            ins.then_inc(s["normed"], 1)
                        if step == 2:
                            dve.wait_ge(s["f_done"], i + 1)
                            for c in range(C):
                                hb = k.h[:, c, bass.ds(i, 1), :].rearrange("p o t -> p (o t)")
                                if d == 0:
                                    ins = nc.vector.scalar_tensor_tensor(out=hb, in0=pm[:, c, 0:T], scalar=lnc[:, 2, c:c + 1], in1=hb, op0=ALU.add, op1=ALU.add)
                                else:
                                    ins = nc.vector.tensor_tensor(hb, hb, pm[:, c, T - 1::-1], ALU.add)
                            ins.then_inc(s["f_out"], 1)

                    def body(i, v, before, after):
                        hlink = per_image(dve, s["head_link"], i + 1, 10)
                        for n in range(NCH):
                            j, q = n // QN, n % QN
                            dve.wait_ge(s["hc_done"], Turn(i, NCH, 2)(n - 1))
                            for m in range(4):
                                dve.wait_ge(s["b_done"], Turn(i, 4 * NCH)(4 * n + m + 1))
                                b2 = pb[:, 2 * (m % 2):2 * (m % 2) + 2, 0:T]
                                nc.vector.tensor_tensor(hs[:, n % 2, 2 * m:2 * m + 2, :], b2, dtu2[:, v, j:j + 1, :].broadcast_to([P, 2, T]), ALU.mult).then_inc(s["b_free"], 1)
                            dve.wait_ge(s["b_free"], Turn(i, 4 * NCH, 2)(4 * n + 4))
                            dve.wait_ge(s["da_done"], Turn(i, NCH)(n + 1))
                            h1 = hs[:, n % 2].rearrange("p n t -> p (n t)")
                            nc.vector.tensor_tensor_scan(h1, da[:, n % 2].rearrange("p n t -> p (n t)"), h1, 0.0, ALU.mult, ALU.add).then_inc(s["h_done"], 1)
                            if n:
                                halve(i, n - 1)
                            if q == 2 and j:
                                out_chunk(i, v, j - 1)
                            if n == 2 and before:
                                out_chunk(i - 1, 1 - v, DJ - 1)
                            if before and n in (5, 7, 8):
                                tail(i - 1, {5: 0, 7: 1, 8: 2}[n])
                            if after:
                                if n == 10:
                                    conv(i + 1, hlink)
                                if n == 12:
                                    split(i + 1, hlink)
                                if n == 13:
                                    take_dt(i + 1, 1 - v)
                                if n == 14:
                                    soften(i + 1, 1 - v, hlink)
                        halve(i, NCH - 1)

                    hlink = per_image(dve, s["head_link"], 0, 10)
                    conv(0, hlink)
                    split(0, hlink)
                    take_dt(0, 0)
                    soften(0, 0, hlink)
                    images(dve, body)
                    out_chunk(B - 1, 1, DJ - 1)
                    for step in range(3):
                        tail(B - 1, step)
            clear(nc, k, s.values())



def section_adapters(nc, k, w_g, w_d, b_d, w_u, b_u):
    E, BN = 8, 64
    HC = E * BN // P
    with ExitStack() as ctx:
        sb = lambda name, shape, dt=F32: ctx.enter_context(nc.sbuf_tensor("ada_" + name, shape, dt))
        ps = lambda name, shape: ctx.enter_context(nc.psum_tensor("ada_" + name, shape, F32))
        wg, wd, wu = sb("wg", [P, C, E]), sb("wd", [P, C, E * BN]), sb("wu", [P, HC, D])
        bd, bu = sb("bd", [P, HC]), sb("bu", [P, C, E])
        iota = sb("iota", [P, E])
        pool_ = sb("pool", [P, C, B])
        pb_ = sb("poolb", [P, C, P])
        gw = sb("gw", [P, B, E])
        lg, ex = sb("lg", [P, E]), sb("ex", [P, E])
        st = sb("st", [P, 4])
        mx, ix, fx = sb("mx", [P, 8]), sb("ix", [P, 8], U32), sb("fx", [P, 2])
        hot = sb("hot", [P, 2, E])
        bias = sb("bias", [P, C, B])
        hid = sb("hid", [P, 2, HC, T])
        junk = sb("junk", [P, E])
        gcol = sb("gcol", [P, B, HC])
        pl = ps("pl", [P, BANK])
        ph = ps("ph", [P, 2, 2, BANK])
        s = {n: signal(nc, ctx, "ada_" + n) for n in "w_in pooled logits sm_in sm_out ready h_done h_act h_scaled y_done y_free".split()}
        ln_tensor, ln_scalar, ln_vector = layer_norm(nc, k, None)
        with nc.Block() as block:
            @block.sync
            def _(sp):
                for dst, src in ((wg[:], w_g), (wd[:], w_d), (wu[:], w_u), (bd[:], b_d), (bu[:], b_u), (iota[:], k.iota[0:E].partition_broadcast(P))):
                    sp.dma_start(dst, src).then_inc(s["w_in"], 16)

            @block.tensor
            def _(pe):
                ln_tensor(pe)
                pe.wait_ge(s["w_in"], 16 * 6)
                with pe.Fori(0, B) as i:
                    pe.wait_ge(s["pooled"], i + 1)
                    for c in range(C):
                        ins = nc.tensor.matmul(pl[:, 0:E], pb_[:, c, :], wg[:, c, :], start=(c == 0), stop=(c == C - 1))
                    ins.then_inc(s["logits"], 1)
                pe.wait_ge(s["ready"], 1)
                pe.wait_ge(s["y_free"], 1)
                with pe.Fori(0, B) as i:
                    xb = [k.x[:, c, bass.ds(i, 1), :] for c in range(C)]
                    for half in range(2):
                        pe.wait_ge(s["h_act"], 2 * i + half + 1)
                        for o in range(2):
                            j = 2 * half + o
                            for c in range(C):
                                ins = nc.tensor.matmul(ph[:, half, o, 0:T], wd[:, c, j * P:j * P + P], xb[c], start=(c == 0), stop=(c == C - 1))
                        ins.then_inc(s["h_done"], 1)
                    pe.wait_ge(s["h_scaled"], i + 1)
                    pe.wait_ge(s["y_free"], i + 1)
                    for c in range(C):
                        for j in range(HC):
                            ins = nc.tensor.matmul(k.ln_ps[:, c, 0:T], wu[:, j, c * P:c * P + P], hid[:, 0, j, :], start=(j == 0), stop=(j == HC - 1))
                    ins.then_inc(s["y_done"], 1)

            @block.scalar
            def _(act):
                ln_scalar(act)
                with act.Fori(0, B) as i:
                    act.wait_ge(s["sm_in"], i + 1)
                    nc.scalar.activation(ex[:], lg[:], ACT.Exp).then_inc(s["sm_out"], 1)
                act.wait_ge(s["w_in"], 16 * 6)
                act.sem_inc(s["h_act"], 2)
                with act.Fori(0, B) as i:
                    act.wait_ge(s["y_free"], i + 1)
                    for j in range(HC):
                        act.wait_ge(s["h_done"], 2 * i + j // 2 + 1)
                        ins = nc.scalar.activation(hid[:, 0, j, :], ph[:, j // 2, j % 2, 0:T], ACT.Gelu, bias=bd[:, j:j + 1])
                        if j % 2:
                            ins.then_inc(s["h_act"], 1)

            @block.vector
            def _(dve):
                ln_vector(dve)
                dve.wait_ge(k.ln_free, B + 1)
                link = Link(dve, k.dve_link)
                dve.wait_ge(s["w_in"], 16 * 6)
                for c in range(C):
                    ins = nc.vector.tensor_reduce(pool_[:, c, :], k.x[:, c], AX, ALU.add)
                link(ins)
                link(nc.vector.tensor_scalar_mul(pool_[:], pool_[:], 1.0 / T))
                with dve.Fori(0, B) as i:
                    link.enter(i, 19)
                    link(nc.vector.tensor_copy(pb_[:], pool_[:, :, bass.ds(i, 1)].broadcast_to([P, C, P])))
                    dve.sem_inc(s["pooled"], 1)
                    dve.wait_ge(s["logits"], i + 1)
                    link(nc.vector.tensor_reduce(st[:, 0:1], pl[:, 0:E], AX, ALU.max))
                    nc.vector.tensor_scalar(lg[:], pl[:, 0:E], st[:, 0:1], None, ALU.subtract).then_inc(s["sm_in"], 1)
                    dve.wait_ge(s["sm_out"], i + 1)
                    link(nc.vector.tensor_reduce(st[:, 1:2], ex[:], AX, ALU.add))
                    link(nc.vector.reciprocal(st[:, 1:2], st[:, 1:2]))
                    link(nc.vector.tensor_scalar(ex[:], ex[:], st[:, 1:2], None, ALU.mult))
                    settle(dve, k)
                    link(nc.vector.max(mx[:], ex[:]))
                    settle(dve, k)
                    link(nc.vector.max_index(ix[:], mx[:], ex[:]))
                    link(nc.vector.tensor_tensor(st[:, 2:3], mx[:, 0:1], mx[:, 1:2], ALU.add))
                    link(nc.vector.tensor_scalar_add(st[:, 2:3], st[:, 2:3], 1e-8))
                    link(nc.vector.reciprocal(st[:, 2:3], st[:, 2:3]))
                    link(nc.vector.tensor_copy(fx[:], ix[:, 0:2]))
                    for j in range(2):
                        link(nc.vector.tensor_scalar(hot[:, j], iota[:], fx[:, j:j + 1], mx[:, j:j + 1], ALU.is_equal, ALU.mult))
                    link(nc.vector.tensor_tensor(hot[:, 0], hot[:, 0], hot[:, 1], ALU.add))
                    g = gw[:, bass.ds(i, 1), :].rearrange("p o e -> p (o e)")
                    link(nc.vector.tensor_scalar(hot[:, 1], hot[:, 0], st[:, 2:3], None, ALU.mult))
                    link(nc.vector.tensor_copy(g, hot[:, 1]))
                    for c in range(C):
                        link(nc.vector.tensor_tensor_reduce(junk[:], bu[:, c, :], hot[:, 1], 1.0, 0.0, ALU.mult, ALU.add, st[:, 2 + c:3 + c]))
                    link(nc.vector.tensor_copy(bias[:, :, bass.ds(i, 1)].rearrange("p c o -> p (c o)"), st[:, 2:4]))
                link.leave(B)
                for half in range(2):
                    src = gw[64 * half:64 * half + 64].rearrange("p b (j e) -> p b j e", e=2)
                    link(nc.vector.tensor_copy(gcol[64 * half:64 * half + 64], src[:, :, :, half]))
                dve.sem_inc(s["y_free"], 1)
                dve.sem_inc(s["ready"], 1)
                with dve.Fori(0, B) as i:
                    link.enter(i, 1)
                    dve.wait_ge(s["h_act"], 2 * i + 4)
                    g = gcol[:, bass.ds(i, 1), :].rearrange("p o j -> p j o").broadcast_to([P, HC, T])
                    nc.vector.tensor_tensor(hid[:, 0], hid[:, 0], g, ALU.mult).then_inc(s["h_scaled"], 1)
                    dve.wait_ge(s["y_done"], i + 1)
                    hb = k.h[:, :, bass.ds(i, 1), :].rearrange("p c o t -> p c (o t)")
                    link(nc.vector.tensor_tensor(hb, hb, k.ln_ps[:, :, 0:T], ALU.add))
                    bb = bias[:, :, bass.ds(i, 1)].broadcast_to([P, C, T])
                    nc.vector.tensor_tensor(hb, hb, bb, ALU.add).then_inc(s["y_free"], 1)
                link.leave(B)
        clear(nc, k, s.values())


def section_switch(nc, k, w_r, b_r, w_1, b_1, w_2, b_2):
    E, HID = 32, 64
    EP = E // 2
    with ExitStack() as ctx:
        sb = lambda name, shape, dt=F32: ctx.enter_context(nc.sbuf_tensor("sw_" + name, shape, dt))
        ps = lambda name, shape: ctx.enter_context(nc.psum_tensor("sw_" + name, shape, F32))
        r = route_tiles(sb, E)
        wr, w1, w2 = sb("wr", [P, C, E]), sb("w1", [P, EP, C, P]), sb("w2", [P, EP, D])
        b1, b2 = sb("b1", [P, EP]), sb("b2", [E, D])
        gates = sb("gates", [E, B, T])
        gb = sb("gb", [P, EP, T])
        hr = sb("hr", [P, 2, T])
        hid = sb("hid", [P, 2, T])
        yr = sb("yr", [P, C, T])
        ph = ps("ph", [P, 2, BANK])
        py = ps("py", [P, C, BANK])
        p_l, p_t = ph[:, 0, :], ph[:, 1, :]
        g_dram = nc.dram_tensor("sw_gates_dram", [E, B, T], F32).ap()
        s = {n: signal(nc, ctx, "sw_" + n) for n in ROUTE_SIGS + "r_in g_out gb_in gb_free u_done u_free h_act h_done y_done y_act y_free".split()}
        ln_tensor, ln_scalar, ln_vector = layer_norm(nc, k, None)
        pool_body, tensor_body, scalar_body, vector_body, links = route_images(nc, k, s, r, E, wr, "one", p_l, p_t, gates, None)
        with nc.Block() as block:
            @block.sync
            def _(sp):
                for dst, src in ((wr[:], w_r), (r["rb"][:], b_r.partition_broadcast(P)), (r["iota"][:], k.iota[0:E].partition_broadcast(P)),
                                 (w1[:], w_1), (w2[:], w_2), (b1[:], b_1), (b2[:], b_2)):
                    sp.dma_start(dst, src).then_inc(s["r_in"], 16)
                sp.wait_ge(s["t_free"], B + 1)
                sp.dma_start(g_dram, gates[:]).then_inc(s["g_out"], 16)
                sp.wait_ge(s["g_out"], 16)
                with sp.Fori(0, B) as i:
                    sp.wait_ge(s["gb_free"], i * EP + 2)
                    for half in range(2):
                        src = g_dram.rearrange("(q o) b t -> o b q t", o=2)[half, bass.ds(i, 1)].rearrange("u q t -> (u q) t")
                        sp.dma_start(gb[64 * half:64 * half + 64], src.partition_broadcast(64)).then_inc(s["gb_in"], 16)

            @block.gpsimd
            def _(pool):
                pool.wait_ge(k.ln_free, B + 1)
                with pool.Fori(0, B) as i:
                    pool_body(pool, i)

            @block.tensor
            def _(pe):
                ln_tensor(pe)
                pe.wait_ge(s["r_in"], 16 * 7)
                with pe.Fori(0, B) as i:
                    tensor_body(pe, i)
                pe.wait_ge(s["t_free"], B + 1)
                pe.wait_ge(s["l_free"], B + 1)
                with pe.Fori(0, B) as i:
                    uf, hd = Turn(i, EP, 2), Turn(i, EP)
                    gi = gates[:, bass.ds(i, 1), :].rearrange("e o t -> e (o t)")

                    def second(q):
                        pe.wait_ge(s["h_done"], hd(q + 1))
                        if q == 0:
                            pe.wait_ge(s["y_free"], i + 1)
                            for c in range(C):
                                nc.tensor.matmul(py[:, c, 0:T], b2[:, c * P:c * P + P], gi, start=True, stop=False)
                        for c in range(C):
                            ins = nc.tensor.matmul(py[:, c, 0:T], w2[:, q, c * P:c * P + P], hid[:, q % 2, :], start=False, stop=(q == EP - 1))
                        return ins

                    for q in range(EP):
                        pe.wait_ge(s["u_free"], uf(q - 1))
                        for c in range(C):
                            ins = nc.tensor.matmul(ph[:, q % 2, 0:T], w1[:, q, c, :], k.x[:, c, bass.ds(i, 1), :], start=(c == 0), stop=(c == C - 1))
                        ins.then_inc(s["u_done"], 1)
                        if q:
                            second(q - 1)
                    second(EP - 1).then_inc(s["y_done"], 1)

            @block.scalar
            def _(act):
                ln_scalar(act)
                act.sem_inc(s["t_free"], 1)
                with act.Fori(0, B) as i:
                    scalar_body(act, i)
                act.sem_inc(s["u_free"], 2)
                act.wait_ge(s["r_in"], 16 * 7)
                with act.Fori(0, B) as i:
                    for q in range(EP):
                        act.wait_ge(s["u_done"], i * EP + q + 1)
                        act.wait_ge(s["gb_free"], i * EP + q + 1)
                        nc.scalar.activation(hr[:, q % 2, :], ph[:, q % 2, 0:T], ACT.Relu, bias=b1[:, q:q + 1]).then_inc(s["u_free"], 1)
                    act.wait_ge(s["y_done"], i + 1)
                    nc.scalar.activation(yr[:], py[:, :, 0:T], ACT.Relu).then_inc(s["y_act"], 1)

            @block.vector
            def _(dve):
                ln_vector(dve)
                dve.wait_ge(k.ln_free, B + 1)
                link = Link(dve, k.dve_link)
                dve.sem_inc(s["l_free"], 1)
                dve.sem_inc(s["xb_free"], 1)
                dve.wait_ge(s["r_in"], 16 * 7)
                with dve.Fori(0, B) as i:
                    link.enter(i, links)
                    vector_body(dve, link, i)
                link.leave(B)
                dve.sem_inc(s["gb_free"], 2)
                dve.sem_inc(s["y_free"], 1)
                with dve.Fori(0, B) as i:
                    dve.wait_ge(s["gb_in"], i * 32 + 32)
                    for q in range(EP):
                        dve.wait_ge(s["u_free"], i * EP + q + 3)
                        nc.vector.tensor_tensor(hid[:, q % 2, :], hr[:, q % 2, :], gb[:, q, :], ALU.mult).then_inc(s["h_done"], 1)
                        dve.wait_ge(s["h_done"], i * EP + q + 1)
                        dve.sem_inc(s["gb_free"], 1)
                    dve.wait_ge(s["y_act"], i + 1)
                    hb = k.h[:, :, bass.ds(i, 1), :].rearrange("p c o t -> p c (o t)")
                    nc.vector.tensor_tensor(hb, hb, yr[:], ALU.add).then_inc(s["y_free"], 1)
        clear(nc, k, s.values())


def build(nc, a, out, last):
    with ExitStack() as ctx:
        sb = lambda name, shape, dt=F32: ctx.enter_context(nc.sbuf_tensor(name, shape, dt))
        k = Kit()
        (k.const_set, k.loads, k.dve_link, k.act_link, k.pool_link, k.ln_free, k.ln_mean, k.ln_var, k.ln_sqd, k.ln_cent,
         k.ln_std, k.ffn_out, k.stored, k.passed) = [signal(nc, ctx, name) for name in (
             "const_set", "loads", "dve_link", "act_link", "pool_link", "ln_free", "ln_mean", "ln_var", "ln_sqd", "ln_cent",
             "ln_std", "ffn_out", "stored", "passed")]
        k.ln_log = signal(nc, ctx, "ln_log")
        k.shared = [k.dve_link, k.act_link, k.pool_link, k.ln_free, k.ln_mean, k.ln_var, k.ln_sqd, k.ln_cent, k.ln_std, k.ln_log, k.ffn_out]
        k.h = sb("h", [P, C, B, T])
        k.x = sb("x", [P, C, B, T])
        k.xb = sb("xb", [P, C, TP])
        k.cls = sb("cls", [P, C])
        k.ones = sb("ones", [P, TP])
        k.mean = sb("mean", [P, P])
        k.ident = sb("ident", [P, P])
        k.eps = sb("eps", [P, 2])
        k.junk = sb("junk", [P, P])
        k.ln_cen, k.ln_sq, k.ln_rstd = sb("ln_cen", [P, C, T]), sb("ln_sq", [P, C, T]), sb("ln_rstd", [P, T])
        k.ln_ps = ctx.enter_context(nc.psum_tensor("ln_ps", [P, 2, BANK], F32))
        section_constants(nc, k, a["cls"])
        section_tokens(nc, k, a["img"], a["wa"], [None, a["wd3"], a["wd2"], a["wd1"]], a["tok_b"])
        if last >= 1:
            section_memory(nc, k, a["mem_wqv"], a["mem_wk"], a["mem_wg"], a["mem_bg"], a["mem_wo"])
        if last >= 2:
            section_moe(nc, k, "moe0", 8, "softmax2", a["moe0_r"], a["moe0_up"], a["moe0_down"], a["iota"], scale=a["moe0_scale"])
        con = {"cst": a["cst"], "ind": a["ind"]}
        if last >= 3:
            section_attention(nc, k, "lat", True, 1.0 / DH ** 0.5, con, None, None, None, a["lat_o"],
                              fold=(a["lat_qd"], a["lat_kd"], a["lat_vd"], a["lat_up"]), rope=a["rope"])
        if last >= 4:
            section_moe(nc, k, "moe1", 16, "sigmoid1", a["moe1_r"], a["moe1_up"], a["moe1_down"], a["iota"], shared=True)
        if last >= 5:
            section_mamba(nc, k, {"sel": a["sel"]}, [{n: a["ssm_%s_%s" % (n, d)] for n in ("win", "wx", "wdt", "wout", "wfu", "cols", "alog", "ln")} for d in "fb"],
                          a["ssm_bfuse"])
        k.iota = a["iota"]
        if last >= 6:
            section_adapters(nc, k, a["ada_wg"], a["ada_wd"], a["ada_bd"], a["ada_wu"], a["ada_bu"])
        if last >= 7:
            section_attention(nc, k, "duo", False, 1.0 / DH ** 0.5, con, a["duo_q"], a["duo_k"], a["duo_v"], a["duo_o"],
                              w_k2=a["duo_k2"], alpha=a["duo_alpha"])
        if last >= 8:
            section_switch(nc, k, a["sw_wr"], a["sw_br"], a["sw_w1"], a["sw_b1"], a["sw_w2"], a["sw_b2"])
        with nc.Block() as block:
            @block.sync
            def _(sp):
                sp.dma_start(out, k.h[:]).then_inc(k.stored, 16)
                sp.wait_ge(k.stored, 16)


def kmajor(w):
    K, M = w.shape
    return np.ascontiguousarray(w.reshape(K // P, P, M).transpose(1, 0, 2))


def kmajors(w):
    E, K, M = w.shape
    return np.ascontiguousarray(w.reshape(E, K // P, P, M).transpose(0, 2, 1, 3))


def pad_rows(w):
    M = w.shape[1]
    q = w.reshape(G, J4, DH, M)
    return np.concatenate([q, np.zeros_like(q)], axis=2).reshape(G, P, M).transpose(1, 0, 2)


def pad_cols(w):
    K = w.shape[0]
    q = w.reshape(K, HEADS, DH)
    return kmajor(np.concatenate([q, np.zeros_like(q)], axis=2).reshape(K, HEADS * 32))


def rope_tables():
    freq = (1.0 / np.float32(10000.0) ** (np.arange(0, 8, 2, dtype=np.float32) / np.float32(8))).astype(np.float32)
    ang = np.arange(T, dtype=np.float32)[:, None] * freq[None, :]
    ang = np.concatenate([ang, ang], axis=1).T
    cos, sin = np.ones((32, T), np.float32), np.zeros((32, T), np.float32)
    cos[8:16] = np.cos(ang)
    sin[8:16] = np.sin(ang) * np.array([-1, 1] * 4, np.float32)[:, None]
    return np.stack([np.tile(cos, (4, 1)), np.tile(sin, (4, 1))], axis=1)


def shape_constants():
    c = np.zeros((6, P, P), np.float32)
    c[0] = -np.eye(P)
    for j in range(4):
        c[1, 32 * j, 32 * j + 16] = -1
        c[2, 32 * j, 32 * j + 17] = -1
        c[3, 32 * j + 16, 32 * j:32 * j + 32] = 1
    c[4] = np.triu(np.full((P, P), NEG, np.float32), 1)
    c[5] = c[4].T
    ind = np.zeros((P, 2), np.float32)
    ind[16::32, 0] = 1
    ind[17::32, 1] = 1
    return c.transpose(1, 0, 2), ind


def layouts(i):
    a = {}
    a["img"] = i["x"].reshape(2, 4, IMG, 32, 8).transpose(1, 3, 0, 4, 2).reshape(P, 2, 8, IMG)
    a["cls"] = i["cls_tok"].reshape(C, P).T
    a["wa"] = i["L0_tok_Wa"].reshape(32, 32).T
    for name, n in (("Wd1", 32), ("Wd2", 64), ("Wd3", 128)):
        r = n // 32
        a["w" + name[1:].lower()] = i["L0_tok_" + name].reshape(3, n, 32, r, 3).transpose(2, 4, 0, 3, 1).reshape(32, 3, 3 * r * n)
    a["tok_b"] = np.concatenate([i["L0_tok_bd1"], i["L0_tok_bd2"], i["L0_tok_bd3"], i["L0_tok_ba"]])
    a["mem_wqv"] = kmajor(np.concatenate([i["L0_attn_Wq"].T, i["L0_attn_Wv"].T], axis=1))
    a["mem_wk"] = kmajor(i["L0_attn_Wk"].T)
    a["mem_wg"] = i["L0_attn_Wg"].reshape(C, P).T
    a["mem_bg"] = i["L0_attn_bg"]
    a["mem_wo"] = i["L0_attn_Wo"].T
    a["iota"] = np.arange(32, dtype=np.float32)
    a["moe0_r"] = kmajor(i["L0_ffn_w_router"].T)
    a["moe0_scale"] = i["L0_ffn_norm_scale"].reshape(C, P).T
    a["moe0_up"] = kmajors(i["L0_ffn_w_up"].transpose(0, 2, 1))
    a["moe0_down"] = kmajors(i["L0_ffn_w_down"].transpose(0, 2, 1))
    a["moe1_r"] = kmajor(i["L1_ffn_w_router"].T)
    gu = i["L1_ffn_gate_up_proj"]
    shared_up = np.concatenate([i["L1_ffn_w_up"].T, i["L1_ffn_w_gate"].T], axis=1)
    a["moe1_up"] = kmajors(np.concatenate([np.concatenate([gu[:, :, 512:], gu[:, :, :512]], axis=2), shared_up[None]]))
    a["moe1_down"] = kmajors(np.concatenate([i["L1_ffn_down_proj"], i["L1_ffn_w_down"].T[None]]))
    down = lambda w: w.T.reshape(HEADS, 64, D).transpose(1, 0, 2)
    for n in "qkv":
        a["lat_%sd" % n] = down(i["L1_attn_W%s_down" % n])
    turned = np.arange(8) ^ 1
    gap = np.zeros((64, 16), np.float32)
    ups = []
    for n in "qk":
        uc, ue = i["L1_attn_W%s_up_c" % n], i["L1_attn_W%s_up_e" % n]
        ups += [uc, ue, gap, uc, ue[:, turned], gap]
    a["lat_up"] = np.concatenate(ups + [i["L1_attn_Wv_up"]], axis=1)
    a["lat_o"] = pad_rows(i["L1_attn_Wc"])
    a["rope"] = rope_tables()
    a["cst"], a["ind"] = shape_constants()
    per = lambda v: v.reshape(DJ, P, -1).transpose(1, 0, 2)
    for n, d in enumerate("fb"):
        w = {x: i["L2_attn_%s_%s" % (x, d)] for x in "Win convw convb Wx Wdt bdt Alog Dp Wout ln_g ln_b".split()}
        a["ssm_win_" + d] = kmajor(w["Win"].T)
        wx = w["Wx"].T
        a["ssm_wx_" + d] = kmajor(np.concatenate([wx[:, RK:], wx[:, :RK]], axis=1))
        a["ssm_wdt_" + d] = w["Wdt"].T
        a["ssm_wout_" + d] = kmajor(w["Wout"].T)
        a["ssm_wfu_" + d] = kmajor(i["L2_attn_Wfuse"][:, n * D:(n + 1) * D].T)
        a["ssm_cols_" + d] = np.concatenate([per(w[x]) for x in ("convw", "convb", "bdt", "Dp")], axis=2)
        a["ssm_alog_" + d] = per(w["Alog"])
        a["ssm_ln_" + d] = np.stack([w["ln_g"].reshape(C, P).T, w["ln_b"].reshape(C, P).T], axis=1)
    a["ssm_bfuse"] = i["L2_attn_bfuse"].reshape(C, P).T
    a["sel"] = np.tile(np.eye(NS_, dtype=np.float32), (3, 1))
    a["ada_wg"] = kmajor(i["L2_ffn_gate_w"].T)
    a["ada_wd"] = kmajor(i["L2_ffn_down_w"].reshape(512, D).T)
    a["ada_bd"] = i["L2_ffn_down_b"].reshape(4, P).T
    a["ada_wu"] = kmajor(i["L2_ffn_up_w"].transpose(0, 2, 1).reshape(512, D))
    a["ada_bu"] = i["L2_ffn_up_b"].reshape(8, C, P).transpose(2, 1, 0)
    a["duo_q"], a["duo_k"], a["duo_k2"] = (pad_cols(i["L3_attn_W_" + n].T) for n in ("Q", "K", "K_prime"))
    a["duo_v"] = kmajor(i["L3_attn_W_V"].T)
    a["duo_o"] = pad_rows(i["L3_attn_W_O"].T)
    a["duo_alpha"] = i["L3_attn_alpha"].reshape(1)
    a["sw_wr"], a["sw_br"] = kmajor(i["L3_ffn_router_w"].T), i["L3_ffn_router_b"]
    a["sw_w1"] = i["L3_ffn_weights1"].reshape(16, 2, C, P, 64).transpose(3, 0, 2, 1, 4).reshape(P, 16, C, P)
    a["sw_b1"] = i["L3_ffn_bias1"].reshape(16, P).T
    a["sw_w2"] = i["L3_ffn_weights2"].reshape(16, P, D).transpose(1, 0, 2)
    a["sw_b2"] = i["L3_ffn_bias2"]
    return {n: np.ascontiguousarray(v) for n, v in a.items()}


LAST = 9


def kernel(**inputs):
    import concourse.bacc as _bacc
    from concourse.bass_utils import run_bass_kernel_spmd as _run

    nc = _bacc.Bacc("TRN2", target_bir_lowering=False, num_devices=1)
    arrays = layouts({n: np.asarray(v) for n, v in inputs.items()})
    aps = {n: nc.dram_tensor("in_" + n, v.shape, mybir.dt.from_np(v.dtype), kind="ExternalInput").ap() for n, v in arrays.items()}
    out = nc.dram_tensor("out", (P, C, B, T), F32, kind="ExternalOutput").ap()
    build(nc, aps, out, LAST)
    r = _run(nc, [{"in_" + n: v for n, v in arrays.items()}], core_ids=[0])
    return r.results[0]["out"].transpose(2, 3, 1, 0).reshape(B, T, D)
```
